# Optimizing a Trainium2 kernel written in Bass

```python
import numpy as np
import jax
import jax.numpy as jnp

def _softmax(x, axis=-1):
    return jax.nn.softmax(x, axis=axis)

def _gelu(x):
    return jax.nn.gelu(x, approximate=True)

def _silu(x):
    return jax.nn.silu(x)

def _sigmoid(x):
    return jax.nn.sigmoid(x)

def _layernorm(x, axis=-1, eps=1e-05):
    m = jnp.mean(x, axis=axis, keepdims=True)
    v = jnp.var(x, axis=axis, keepdims=True)
    return (x - m) / jnp.sqrt(v + eps)

def _scatter_add(tgt, idx, src, axis=0):
    return tgt.at[idx].add(src)

def _segment_sum(src, seg, n):
    return jax.ops.segment_sum(src, seg, n)
kernel_name = 'mk_dlrm_tower_d1_rec_r8_764e8f'

def setup_inputs(seed: int=0):
    np.random.seed(seed)
    _w = jnp.asarray

    def _rec_inputs():
        import jax
        import jax.numpy as jnp
        _tk = jax.random.key(seed)
        ids = jnp.stack([jax.random.randint(jax.random.fold_in(_tk, 200 + f), (2048,), 0, v, jnp.int32) for f, v in enumerate([12500, 12500, 1000, 1000, 12500, 125000, 1000, 12500, 1000, 1000, 12500, 12500, 1000, 12500, 1250, 1000, 12500, 1250, 12500, 1000, 1250, 1250, 1000, 1000, 1000, 1000])], axis=1)
        tbl_0 = 0.05 * jax.random.normal(jax.random.fold_in(_tk, 500 + 0), (12500, 128), jnp.float32)
        tbl_1 = 0.05 * jax.random.normal(jax.random.fold_in(_tk, 500 + 1), (12500, 128), jnp.float32)
        tbl_2 = 0.05 * jax.random.normal(jax.random.fold_in(_tk, 500 + 2), (1000, 128), jnp.float32)
        tbl_3 = 0.05 * jax.random.normal(jax.random.fold_in(_tk, 500 + 3), (1000, 128), jnp.float32)
        tbl_4 = 0.05 * jax.random.normal(jax.random.fold_in(_tk, 500 + 4), (12500, 128), jnp.float32)
        tbl_5 = 0.05 * jax.random.normal(jax.random.fold_in(_tk, 500 + 5), (125000, 128), jnp.float32)
        tbl_6 = 0.05 * jax.random.normal(jax.random.fold_in(_tk, 500 + 6), (1000, 128), jnp.float32)
        tbl_7 = 0.05 * jax.random.normal(jax.random.fold_in(_tk, 500 + 7), (12500, 128), jnp.float32)
        tbl_8 = 0.05 * jax.random.normal(jax.random.fold_in(_tk, 500 + 8), (1000, 128), jnp.float32)
        tbl_9 = 0.05 * jax.random.normal(jax.random.fold_in(_tk, 500 + 9), (1000, 128), jnp.float32)
        tbl_10 = 0.05 * jax.random.normal(jax.random.fold_in(_tk, 500 + 10), (12500, 128), jnp.float32)
        tbl_11 = 0.05 * jax.random.normal(jax.random.fold_in(_tk, 500 + 11), (12500, 128), jnp.float32)
        tbl_12 = 0.05 * jax.random.normal(jax.random.fold_in(_tk, 500 + 12), (1000, 128), jnp.float32)
        tbl_13 = 0.05 * jax.random.normal(jax.random.fold_in(_tk, 500 + 13), (12500, 128), jnp.float32)
        tbl_14 = 0.05 * jax.random.normal(jax.random.fold_in(_tk, 500 + 14), (1250, 128), jnp.float32)
        tbl_15 = 0.05 * jax.random.normal(jax.random.fold_in(_tk, 500 + 15), (1000, 128), jnp.float32)
        tbl_16 = 0.05 * jax.random.normal(jax.random.fold_in(_tk, 500 + 16), (12500, 128), jnp.float32)
        tbl_17 = 0.05 * jax.random.normal(jax.random.fold_in(_tk, 500 + 17), (1250, 128), jnp.float32)
        tbl_18 = 0.05 * jax.random.normal(jax.random.fold_in(_tk, 500 + 18), (12500, 128), jnp.float32)
        tbl_19 = 0.05 * jax.random.normal(jax.random.fold_in(_tk, 500 + 19), (1000, 128), jnp.float32)
        tbl_20 = 0.05 * jax.random.normal(jax.random.fold_in(_tk, 500 + 20), (1250, 128), jnp.float32)
        tbl_21 = 0.05 * jax.random.normal(jax.random.fold_in(_tk, 500 + 21), (1250, 128), jnp.float32)
        tbl_22 = 0.05 * jax.random.normal(jax.random.fold_in(_tk, 500 + 22), (1000, 128), jnp.float32)
        tbl_23 = 0.05 * jax.random.normal(jax.random.fold_in(_tk, 500 + 23), (1000, 128), jnp.float32)
        tbl_24 = 0.05 * jax.random.normal(jax.random.fold_in(_tk, 500 + 24), (1000, 128), jnp.float32)
        tbl_25 = 0.05 * jax.random.normal(jax.random.fold_in(_tk, 500 + 25), (1000, 128), jnp.float32)
        _rk = jax.random.fold_in(_tk, 7)
        r_dense_features = -0.000520686 + 1.00062 * jax.random.normal(jax.random.fold_in(_rk, 101), (2048, 128), jnp.float32)
        W_top1 = 0.0405887 * jax.random.normal(jax.random.fold_in(_tk, 801), (607, 512), jnp.float32)
        W_top2 = 0.0441942 * jax.random.normal(jax.random.fold_in(_tk, 802), (512, 256), jnp.float32)
        W_top3 = 0.0625 * jax.random.normal(jax.random.fold_in(_tk, 803), (256, 1), jnp.float32)
        b_top1 = jnp.zeros((512,), jnp.float32)
        b_top2 = jnp.zeros((256,), jnp.float32)
        return (r_dense_features, ids, tbl_0, tbl_1, tbl_2, tbl_3, tbl_4, tbl_5, tbl_6, tbl_7, tbl_8, tbl_9, tbl_10, tbl_11, tbl_12, tbl_13, tbl_14, tbl_15, tbl_16, tbl_17, tbl_18, tbl_19, tbl_20, tbl_21, tbl_22, tbl_23, tbl_24, tbl_25, W_top1, b_top1, W_top2, b_top2, W_top3)
    r_dense_features, ids, tbl_0, tbl_1, tbl_2, tbl_3, tbl_4, tbl_5, tbl_6, tbl_7, tbl_8, tbl_9, tbl_10, tbl_11, tbl_12, tbl_13, tbl_14, tbl_15, tbl_16, tbl_17, tbl_18, tbl_19, tbl_20, tbl_21, tbl_22, tbl_23, tbl_24, tbl_25, W_top1, b_top1, W_top2, b_top2, W_top3 = _rec_inputs()

    def _L0_rec_setup():
        import jax, jax.numpy as jnp
        import numpy as np
        B, F, D = (2048, 26, 128)
        key = jax.random.key(seed)
        k1, k2 = jax.random.split(key)
        dense_features = jax.random.normal(k1, (B, D), dtype=jnp.float32)
        sparse_features = jax.random.normal(k2, (B, F, D), dtype=jnp.float32)
        return {'dense_features': dense_features, 'sparse_features': sparse_features}
    _L0_rec_all = _L0_rec_setup()
    _L0_rec_in = {k: v for k, v in _L0_rec_all.items() if k in ()}
    del _L0_rec_all
    return {'r_dense_features': r_dense_features, 'ids': ids, 'tbl_0': tbl_0, 'tbl_1': tbl_1, 'tbl_2': tbl_2, 'tbl_3': tbl_3, 'tbl_4': tbl_4, 'tbl_5': tbl_5, 'tbl_6': tbl_6, 'tbl_7': tbl_7, 'tbl_8': tbl_8, 'tbl_9': tbl_9, 'tbl_10': tbl_10, 'tbl_11': tbl_11, 'tbl_12': tbl_12, 'tbl_13': tbl_13, 'tbl_14': tbl_14, 'tbl_15': tbl_15, 'tbl_16': tbl_16, 'tbl_17': tbl_17, 'tbl_18': tbl_18, 'tbl_19': tbl_19, 'tbl_20': tbl_20, 'tbl_21': tbl_21, 'tbl_22': tbl_22, 'tbl_23': tbl_23, 'tbl_24': tbl_24, 'tbl_25': tbl_25, 'W_top1': W_top1, 'b_top1': b_top1, 'W_top2': W_top2, 'b_top2': b_top2, 'W_top3': W_top3}

def reference(r_dense_features, ids, tbl_0, tbl_1, tbl_2, tbl_3, tbl_4, tbl_5, tbl_6, tbl_7, tbl_8, tbl_9, tbl_10, tbl_11, tbl_12, tbl_13, tbl_14, tbl_15, tbl_16, tbl_17, tbl_18, tbl_19, tbl_20, tbl_21, tbl_22, tbl_23, tbl_24, tbl_25, W_top1, b_top1, W_top2, b_top2, W_top3):
    import jax
    import jax.numpy as jnp

    def _L0_rec_ref(dense_features, sparse_features):
        import jax, jax.numpy as jnp
        import numpy as np
        B, F, D = (2048, 26, 128)
        combined = jnp.concatenate([dense_features[:, None, :], sparse_features], axis=1)
        interactions = jnp.einsum('bfd,bgd->bfg', combined, combined)
        iu0, iu1 = np.triu_indices(F + 1, k=1)
        interactions_flat = interactions[:, iu0, iu1]
        return jnp.concatenate([dense_features, interactions_flat], axis=1)
    e = jnp.stack([tbl_0[ids[:, 0]], tbl_1[ids[:, 1]], tbl_2[ids[:, 2]], tbl_3[ids[:, 3]], tbl_4[ids[:, 4]], tbl_5[ids[:, 5]], tbl_6[ids[:, 6]], tbl_7[ids[:, 7]], tbl_8[ids[:, 8]], tbl_9[ids[:, 9]], tbl_10[ids[:, 10]], tbl_11[ids[:, 11]], tbl_12[ids[:, 12]], tbl_13[ids[:, 13]], tbl_14[ids[:, 14]], tbl_15[ids[:, 15]], tbl_16[ids[:, 16]], tbl_17[ids[:, 17]], tbl_18[ids[:, 18]], tbl_19[ids[:, 19]], tbl_20[ids[:, 20]], tbl_21[ids[:, 21]], tbl_22[ids[:, 22]], tbl_23[ids[:, 23]], tbl_24[ids[:, 24]], tbl_25[ids[:, 25]]], axis=1)
    z = _L0_rec_ref(r_dense_features, e)
    z = z.reshape(z.shape[0], -1)
    h = jnp.concatenate([z, r_dense_features], axis=1)
    h = jnp.maximum(h @ W_top1 + b_top1, 0.0)
    h = jnp.maximum(h @ W_top2 + b_top2, 0.0)
    y = h @ W_top3
    return y

_drawn_inputs = setup_inputs


def setup_inputs(seed=0):
    import zlib

    import numpy as np

    out = dict(_drawn_inputs(seed))
    spreads = {'b_top1': (0.0, 0.1), 'b_top2': (0.0, 0.1)}
    factors = {}
    for name, (base, spread) in spreads.items():
        noise = np.random.default_rng([zlib.crc32(name.encode()), seed]).standard_normal(out[name].shape)
        drawn = base * np.exp(spread * noise) if base else spread * noise
        out[name] = jnp.asarray(drawn.astype(out[name].dtype))
    for name, factor in factors.items():
        out[name] = (out[name] * factor).astype(out[name].dtype)
    return out
```

```python
from contextlib import ExitStack

import concourse.bass as bass
from concourse import mybir

F32 = mybir.dt.float32
I32 = mybir.dt.int32
ALU = mybir.AluOpType
ACT = mybir.ActivationFunctionType

P = 128


def dlrm_tower(nc, dense, ids, tables, w1, b1, w2, b2, w3, y):
    B, D = dense.shape
    NF = len(tables)
    FEATS = NF + 1
    PAIRS = FEATS * NF // 2
    H1, H2 = w2.shape
    TILES = B // P
    SLOTS = 4
    BLOCKS = TILES // SLOTS
    assert D == P and w1.shape[0] == 2 * D + PAIRS and TILES == SLOTS * BLOCKS

    ROWS = 32
    PER_GROUP = P // ROWS
    FGROUP = 4
    TGROUPS = -(-FEATS // FGROUP)
    BANK_GROUPS = 4
    GBANKS = P // (PER_GROUP * BANK_GROUPS)
    COLS = FEATS - 1
    Q = -(-COLS // PER_GROUP)
    UNIT = 2 * P
    M1, M2 = H1 // P, H2 // P
    HUSES = M1 + M2

    with ExitStack() as ctx:
        def sb(name, shape, dt=F32):
            return ctx.enter_context(nc.sbuf_tensor(name, shape, dt))

        def ps(name, shape, dt=F32):
            return ctx.enter_context(nc.psum_tensor(name, shape, dt))

        def sem(name):
            return ctx.enter_context(nc.semaphore(name))

        idx = sb("idx", [P, TILES + SLOTS, NF], I32)
        idx_slot = sb("idx_slot", [P, SLOTS, NF], I32)
        emb = sb("emb", [P, SLOTS, FEATS, D])
        ones = sb("ones", [P, P])
        ident = sb("ident", [P, P])
        xT = sb("xT", [P, 2, P, ROWS])
        denseT = sb("denseT", [P, 2, UNIT])
        z = sb("z", [P, 2, Q, UNIT])
        wz = sb("wz", [P, Q, H1])
        wd = sb("wd", [P, 3, H1])
        w2s = sb("w2s", [P, M1, H2])
        w3s = sb("w3s", [P, M2])
        b1s = sb("b1s", [P, M1])
        b2s = sb("b2s", [P, M2])
        h1 = sb("h1", [P, M1, UNIT])
        h2 = sb("h2", [P, M2, UNIT])
        y_sb = sb("y_sb", [P, TILES])

        t_ps = [ps(f"t_ps{i}", [P, FGROUP, P]) for i in range(2)]
        g_ps = [ps(f"g_ps{i}", [P, 512]) for i in range(2)]
        h_ps = [ps(f"h_ps{i}", [P, 512]) for i in range(2)]
        y_ps = ps("y_ps", [P, SLOTS])

        idx_landed = sem("idx_landed")
        idx_copied = sem("idx_copied")
        slots_begun = sem("slots_begun")
        idx_pad_zero = sem("idx_pad_zero")
        gathered = [sem(f"gathered{s}") for s in range(SLOTS)]
        dense_landed = [sem(f"dense_landed{s}") for s in range(SLOTS)]
        w_landed = sem("w_landed")
        wd_landed = sem("wd_landed")
        bias_landed = sem("bias_landed")
        ones_set = sem("ones_set")
        ident_ready = sem("ident_ready")
        pads_zero = sem("pads_zero")
        wz_zero = sem("wz_zero")
        wd_summed = sem("wd_summed")
        turned = sem("turned")
        evac = [sem("evac_dve"), sem("evac_act")]
        gram_done = sem("gram_done")
        z_dve = sem("z_dve")
        z_act = sem("z_act")
        h_done = sem("h_done")
        h_ready = sem("h_ready")
        y_done = sem("y_done")
        y_copied = sem("y_copied")
        y_stored = sem("y_stored")

        block = ctx.enter_context(nc.Block())

        dense_tiles = dense.rearrange("(p t) d -> p t d", t=TILES)

        def wz_loads():
            out = []
            row = D
            for f in range(COLS):
                for j in range(PER_GROUP):
                    c0 = f + (j - f) % PER_GROUP
                    n = -(-(COLS - c0) // PER_GROUP)
                    if n <= 0:
                        continue
                    r0 = row + c0 - f
                    src = w1[r0:r0 + PER_GROUP * (n - 1) + 1:PER_GROUP, :]
                    part = ROWS * j + f
                    dst = wz[part:part + 1, c0 // PER_GROUP:c0 // PER_GROUP + n, :]
                    out.append((dst, src.rearrange("(o q) n -> o q n", o=1)))
                row += COLS - f
            return out

        LOADS = wz_loads()
        N_W = 16 * len(LOADS)

        @block.sync
        def _(sp):
            sp.dma_start(idx[:, 0:TILES, :], ids.rearrange("(p t) f -> p t f", t=TILES)).then_inc(idx_landed, 16)

            def load_dense(b, slot, again):
                if again:
                    sp.wait_ge(turned, TGROUPS * SLOTS * (b - 1) + TGROUPS * (slot + 1))
                sp.dma_start(emb[:, slot, 0, :], dense_tiles[:, bass.ds(SLOTS * b + slot, 1), :]
                             .rearrange("p o d -> p (o d)")).then_inc(dense_landed[slot], 16)

            for slot in range(SLOTS):
                load_dense(0, slot, False)
            sp.wait_ge(wz_zero, 1)
            for dst, src in LOADS[::2]:
                sp.dma_start(dst, src).then_inc(w_landed, 16)
            with sp.Fori(1, BLOCKS) as b:
                for slot in range(SLOTS):
                    load_dense(b, slot, True)
            sp.wait_ge(y_copied, TILES // 2)
            sp.dma_start(y.rearrange("(p t) o -> p (t o)", t=TILES), y_sb[:]).then_inc(y_stored, 16)
            sp.wait_ge(y_stored, 16)

        @block.gpsimd
        def _(pool):
            pool.memset(ones[:], 1.0).then_inc(ones_set, 1)
            pool.wait_ge(ones_set, 1)
            pool.affine_select(out=ident[:], in_=ones[:], compare_op=ALU.is_equal, fill=0.0, base=0,
                               pattern=[[-1, P]], channel_multiplier=1).then_inc(ident_ready, 1)

            def gather_block(b):
                for slot in range(SLOTS):
                    pool.wait_ge(idx_copied, SLOTS * b + slot + 1)
                    pool.sem_inc(slots_begun, 1)
                    for f in range(NF):
                        pool.indirect_dma_start(
                            emb[:, slot, f + 1, :], None, tables[f][:, :],
                            bass.IndirectOffsetOnAxis(ap=idx_slot[:, slot, f:f + 1], axis=0)
                        ).then_inc(gathered[slot], 16)

            with pool.Fori(0, BLOCKS) as b:
                gather_block(b)

        @block.tensor
        def _(pe):
            def turn(b, slot, i):
                k = TGROUPS * slot + i
                if i == 0:
                    pe.wait_ge(dense_landed[slot], 16 * (b + 1))
                    pe.wait_ge(gathered[slot], 16 * NF * (b + 1))
                if not (isinstance(b, int) and b == 0 and k < 2):
                    pe.wait_ge(evac[k % 2], TGROUPS * SLOTS // 2 * b + k // 2)
                fs = range(FGROUP * i, min(FGROUP * (i + 1), FEATS))
                for f in fs:
                    last = pe.transpose(t_ps[k % 2][:, f - fs[0], :], emb[:, slot, f, :], ident[:])
                last.then_inc(turned, 1)

            def gram(b, slot, i, first):
                m = GBANKS * slot + i
                if i == 0:
                    pe.wait_ge(evac[0], TGROUPS * SLOTS // 2 * b + -(-TGROUPS * (slot + 1) // 2))
                    pe.wait_ge(evac[1], TGROUPS * SLOTS // 2 * b + TGROUPS * (slot + 1) // 2)
                if not (first and i < 2):
                    pe.wait_ge(z_dve, GBANKS * SLOTS * b + m - 1)
                    pe.wait_ge(z_act, GBANKS * SLOTS * b + m - 1)
                x = xT[:, slot % 2]
                for n in range(BANK_GROUPS):
                    s0 = PER_GROUP * (BANK_GROUPS * i + n)
                    w = PER_GROUP * COLS
                    last = pe.matmul(g_ps[m % 2][:, n * w:(n + 1) * w],
                                     x[:, s0:s0 + PER_GROUP, :].rearrange("d s f -> d (s f)"),
                                     x[:, s0:s0 + PER_GROUP, 1:FEATS], start=True, stop=True)
                last.then_inc(gram_done, 1)

            def layers(b, half, i, first):
                n0 = HUSES * 2 * b + HUSES * half
                if i < M1:
                    if i == 0:
                        if first:
                            pe.wait_ge(w_landed, N_W)
                            pe.wait_ge(wd_summed, 1)
                            pe.wait_ge(bias_landed, 64)
                        pe.wait_ge(z_dve, 2 * GBANKS * (2 * b + half + 1))
                        pe.wait_ge(z_act, 2 * GBANKS * (2 * b + half + 1))
                    if not (first and i < 2):
                        pe.wait_ge(h_ready, n0 + i - 1)
                    out = h_ps[i % 2][:, 0:UNIT]
                    for q in range(Q):
                        pe.matmul(out, wz[:, q, P * i:P * (i + 1)], z[:, half, q, :], start=(q == 0), stop=False)
                    pe.matmul(out, wd[:, 2, P * i:P * (i + 1)], denseT[:, half, :], start=False,
                              stop=True).then_inc(h_done, 1)
                elif i < M1 + M2:
                    c = i - M1
                    if c == 0:
                        pe.wait_ge(h_ready, n0 + M1)
                    for k in range(M1):
                        last = pe.matmul(h_ps[i % 2][:, 0:UNIT], w2s[:, k, P * c:P * (c + 1)], h1[:, k, :],
                                         start=(k == 0), stop=(k == M1 - 1))
                    last.then_inc(h_done, 1)
                elif i == GBANKS - 1:
                    pe.wait_ge(h_ready, n0 + HUSES)
                    if not first:
                        pe.wait_ge(y_copied, 2 * b + half)
                    for tile in range(2):
                        col = 2 * half + tile
                        for c in range(M2):
                            last = pe.matmul(y_ps[:, col:col + 1], h2[:, c, P * tile:P * (tile + 1)],
                                             w3s[:, c:c + 1], start=(c == 0), stop=(c == M2 - 1))
                    last.then_inc(y_done, 1)

            def step(b, slot, do_turn=True, prev=True, unit=True):
                for i in range(GBANKS):
                    if do_turn and i < TGROUPS:
                        turn(b, slot, i)
                    if prev:
                        if slot:
                            gram(b, slot - 1, i, isinstance(b, int) and b == 0 and slot == 1)
                        else:
                            gram(b - 1, SLOTS - 1, i, False)
                    if unit and slot == 1:
                        layers(b - 1, 1, i, False)
                    if unit and slot == 3:
                        layers(b, 0, i, isinstance(b, int) and b == 0)

            pe.wait_ge(ident_ready, 1)
            step(0, 0, prev=False)
            pe.wait_ge(pads_zero, 1)
            step(0, 1, unit=False)
            step(0, 2)
            step(0, 3)
            with pe.Fori(1, BLOCKS) as b:
                for slot in range(SLOTS):
                    step(b, slot)
            step(BLOCKS, 0, do_turn=False)
            step(BLOCKS, 1, do_turn=False, prev=False)

        def copy_turned(engine, b, slot, i, copy):
            k = TGROUPS * slot + i
            engine.wait_ge(turned, TGROUPS * SLOTS * b + k + 1)
            n = min(FGROUP, FEATS - FGROUP * i)
            if i == 0:
                half, tile = slot // 2, slot % 2
                copy(denseT[:, half, P * tile:P * (tile + 1)], t_ps[k % 2][:, 0, :])
            copy(xT[:, slot % 2, :, FGROUP * i:FGROUP * i + n].rearrange("d s f -> d f s"),
                 t_ps[k % 2][:, 0:n, :]).then_inc(evac[k % 2], 1)

        def copy_pairs(engine, b, slot, i, copy, members, done):
            m = GBANKS * slot + i
            half, tile = slot // 2, slot % 2
            engine.wait_ge(gram_done, GBANKS * SLOTS * b + m + 1)
            w = PER_GROUP * COLS
            g = g_ps[m % 2][:, 0:BANK_GROUPS * w].rearrange("r (n s c) -> r n s c", n=BANK_GROUPS, s=PER_GROUP)
            s0 = P * tile + PER_GROUP * BANK_GROUPS * i
            zz = z[:, half, :, s0:s0 + PER_GROUP * BANK_GROUPS].rearrange("r q (n s) -> r s n q", s=PER_GROUP)
            for s in members:
                for j in range(PER_GROUP):
                    nq = -(-(COLS - j) // PER_GROUP)
                    last = copy(zz[ROWS * j:ROWS * (j + 1), s, :, 0:nq],
                                g[ROWS * s:ROWS * (s + 1), :, s, j:j + PER_GROUP * (nq - 1) + 1:PER_GROUP])
            last.then_inc(done, 1)

        @block.vector
        def _(dve):
            dve.memset(idx[:, TILES:, :], 0).then_inc(idx_pad_zero, 1)
            dve.wait_ge(idx_landed, 16)
            for slot in range(SLOTS):
                dve.tensor_copy(idx_slot[:, slot, :], idx[:, slot, :]).then_inc(idx_copied, 1)
            dve.wait_ge(idx_pad_zero, 1)
            dve.memset(wz[:], 0.0).then_inc(wz_zero, 1)
            dve.memset(xT[:, :, :, FEATS:ROWS], 0.0)
            dve.memset(z[2 * ROWS:P, :, Q - 1, :], 0.0).then_inc(pads_zero, 1)

            def step(b, slot, do_turn=True, prev=True):
                for i in range(GBANKS):
                    if do_turn and i < TGROUPS and (TGROUPS * slot + i) % 2 == 0:
                        copy_turned(dve, b, slot, i, dve.tensor_copy)
                    if prev:
                        bb, ss = (b, slot - 1) if slot else (b - 1, SLOTS - 1)
                        copy_pairs(dve, bb, ss, i, dve.tensor_copy, (0, 1), z_dve)
                if do_turn:
                    dve.wait_ge(turned, TGROUPS * SLOTS * b + TGROUPS * (slot + 1))
                    dve.tensor_copy(idx_slot[:, slot, :], idx[:, bass.ds(SLOTS * (b + 1) + slot, 1), :]
                                    .rearrange("p o f -> p (o f)")).then_inc(idx_copied, 1)

            step(0, 0, prev=False)
            dve.wait_ge(wd_landed, 32)
            dve.tensor_tensor(wd[:, 2, :], wd[:, 0, :], wd[:, 1, :], ALU.add).then_inc(wd_summed, 1)
            for slot in range(1, SLOTS):
                step(0, slot)
            with dve.Fori(1, BLOCKS) as b:
                for slot in range(SLOTS):
                    step(b, slot)
            step(BLOCKS, 0, do_turn=False)

        @block.scalar
        def _(act):
            act.dma_start(wd[:, 0, :], w1[0:D, :]).then_inc(wd_landed, 16)
            act.dma_start(wd[:, 1, :], w1[D + PAIRS:2 * D + PAIRS, :]).then_inc(wd_landed, 16)
            act.dma_start(w2s[:], w2.rearrange("(m p) n -> p m n", p=P)).then_inc(bias_landed, 16)
            with nc.allow_non_contiguous_dma(reason="a few hundred words, once"):
                act.dma_start(b1s[:], b1.rearrange("(m p) -> p m", p=P)).then_inc(bias_landed, 16)
                act.dma_start(b2s[:], b2.rearrange("(m p) -> p m", p=P)).then_inc(bias_landed, 16)
                act.dma_start(w3s[:], w3.rearrange("(m p) o -> p (m o)", p=P)).then_inc(bias_landed, 16)
            act.wait_ge(wz_zero, 1)
            for dst, src in LOADS[1::2]:
                act.dma_start(dst, src).then_inc(w_landed, 16)

            def layers(b, half, i, first):
                n0 = HUSES * 2 * b + HUSES * half
                if i < HUSES:
                    if first and i == 0:
                        act.wait_ge(bias_landed, 64)
                    act.wait_ge(h_done, n0 + i + 1)
                    dst, bias = (h1[:, i, :], b1s[:, i:i + 1]) if i < M1 else (h2[:, i - M1, :],
                                                                              b2s[:, i - M1:i - M1 + 1])
                    act.activation(dst, h_ps[i % 2][:, 0:UNIT], ACT.Relu, bias=bias).then_inc(h_ready, 1)
                elif i == GBANKS - 1:
                    act.wait_ge(y_done, 2 * b + half + 1)
                    act.copy(y_sb[:, bass.ds(SLOTS * b + 2 * half, 2)],
                             y_ps[:, 2 * half:2 * half + 2]).then_inc(y_copied, 1)

            def step(b, slot, do_turn=True, prev=True, unit=True):
                for i in range(GBANKS):
                    if do_turn and i < TGROUPS and (TGROUPS * slot + i) % 2 == 1:
                        copy_turned(act, b, slot, i, act.copy)
                    if prev:
                        bb, ss = (b, slot - 1) if slot else (b - 1, SLOTS - 1)
                        copy_pairs(act, bb, ss, i, act.copy, (2, 3), z_act)
                    if unit and slot == 1:
                        layers(b - 1, 1, i, False)
                    if unit and slot == 3:
                        layers(b, 0, i, isinstance(b, int) and b == 0)

            step(0, 0, prev=False)
            step(0, 1, unit=False)
            step(0, 2)
            step(0, 3)
            with act.Fori(1, BLOCKS) as b:
                for slot in range(SLOTS):
                    step(b, slot)
            step(BLOCKS, 0, do_turn=False)
            step(BLOCKS, 1, do_turn=False, prev=False)


def kernel(**inputs):
    import numpy as _np
    import concourse.bacc as _bacc
    from concourse import mybir as _mybir
    from concourse.bass_utils import run_bass_kernel_spmd as _run

    nc = _bacc.Bacc("TRN2", target_bir_lowering=False, num_devices=1)
    arrays, aps = {}, {}
    for name, value in inputs.items():
        a = _np.ascontiguousarray(value)
        arrays[f"in_{name}"] = a
        aps[name] = nc.dram_tensor(f"in_{name}", a.shape, _mybir.dt.from_np(a.dtype), kind="ExternalInput").ap()
    n_tables = aps["ids"].shape[1]
    y = nc.dram_tensor("out_y", (aps["ids"].shape[0], 1), _mybir.dt.float32, kind="ExternalOutput").ap()
    dlrm_tower(nc, aps["r_dense_features"], aps["ids"], [aps[f"tbl_{f}"] for f in range(n_tables)],
               aps["W_top1"], aps["b_top1"], aps["W_top2"], aps["b_top2"], aps["W_top3"], y)
    r = _run(nc, [arrays], core_ids=[0])
    return r.results[0]["out_y"]
```

```python
from contextlib import ExitStack

import concourse.bass as bass
from concourse import mybir

F32 = mybir.dt.float32
F32R = mybir.dt.float32r
F16 = mybir.dt.float16
I32 = mybir.dt.int32
ALU = mybir.AluOpType
ACT = mybir.ActivationFunctionType

P = 128
HOT_TABLE = 1000
HOT_ROWS = 8
MAX_HOT = 6
DVE, SCALAR = 0, 1


def dlrm_tower(nc, dense, ids, tables, w1, b1, w2, b2, w3, y):
    B, D = dense.shape
    NF = len(tables)
    FEATS = NF + 1
    PAIRS = FEATS * NF // 2
    H1, H2 = w2.shape
    TILES = B // P
    UNITS = TILES // 2
    UNIT = 2 * P
    assert D == P and w1.shape[0] == 2 * D + PAIRS and TILES == 2 * UNITS

    HOT = [f for f in range(NF) if tables[f].shape[0] == HOT_TABLE][-MAX_HOT:]
    COLD = [f for f in range(NF) if f not in HOT]
    NH, NC = len(HOT), len(COLD)
    HOT_P = HOT_TABLE // HOT_ROWS
    HOT_RUNS = NH // 2
    STAGES = 5
    assert NH % 2 == 0 and HOT_P <= P

    turned_features = [0] + [f + 1 for f in COLD]
    slot_of = {f: n for n, f in enumerate(turned_features)}
    cold = []
    for f in turned_features:
        if cold and len(cold[-1]) < 4 and cold[-1][-1] == f - 1:
            cold[-1].append(f)
        else:
            cold.append([f])
    COLD_RUNS = [cold, cold[:-1] + [cold[-1][:1], cold[-1][1:]]]
    NCOLD = [len(runs) for runs in COLD_RUNS]
    TURNS = sum(NCOLD)
    FIRST = NCOLD[0] // 2
    GATHERS = [[f - 1 for run in cold[:FIRST] for f in run if f], [f - 1 for run in cold[FIRST:] for f in run]]
    assert len(cold[-1]) > 1 and (TURNS + HOT_RUNS) % 2 == 0

    SPAN = [slice(fields[0], fields[-1] + 1) for fields in GATHERS]

    PIECES = 8
    spaced = [[] for _ in range(PIECES)]
    for n in range(HOT_RUNS):
        spaced[3 * n].append(("hot", n))
    for n in range(NCOLD[0]):
        spaced[n].append(("cold", n))
    eager = [[("hot", n) for n in range(HOT_RUNS)] + [("cold", 0)]] + [[("cold", n)] for n in range(1, NCOLD[0])]
    eager += [[]] * (PIECES - len(eager))
    second = [[("cold", n)] if n < NCOLD[1] else [] for n in range(PIECES)]
    assert NCOLD[1] <= PIECES

    def engine_of(kind, run):
        return DVE if kind == "cold" and run % 2 == 0 else SCALAR

    def number(first_unit):
        out, made = {}, [0, 0]
        for slot, plan in enumerate([eager if first_unit else spaced, second]):
            for piece in plan:
                for kind, run in piece:
                    who = engine_of(kind, run)
                    out[slot, kind, run] = (len(out) % 2, who, made[who])
                    made[who] += 1
        return out, made

    NUMBERED = {first: number(first)[0] for first in (True, False)}
    COPIES = number(False)[1]

    def is_first(u):
        return isinstance(u, int) and u == 0

    def plan_of(u, slot):
        return second if slot else eager if is_first(u) else spaced

    ROWS = 32
    GROUP = P // ROWS
    IN_BANK = 4
    GRAMS = 4
    COLS = FEATS - 1
    WIDE = GROUP * COLS
    Q = -(-COLS // GROUP)
    K1 = Q + 1
    M1, M2 = H1 // P, H2 // P
    HUSES = M1 + M2
    assert GRAMS * 2 * IN_BANK * GROUP == P and ROWS >= FEATS and IN_BANK * WIDE <= 512

    with ExitStack() as ctx:
        def sb(name, shape, dt=F32):
            return ctx.enter_context(nc.sbuf_tensor(name, shape, dt))

        def ps(name, shape, dt=F32):
            return ctx.enter_context(nc.psum_tensor(name, shape, dt))

        def sem(name):
            return ctx.enter_context(nc.semaphore(name))

        idx = sb("idx", [P, TILES + 2, NF], I32)
        idx_slot = sb("idx_slot", [P, 2, NF], I32)
        emb = sb("emb", [P, 2, NC + 1, D])
        ident = sb("ident", [P, P])
        xT = sb("xT", [P, 2, P, ROWS])
        denseT = sb("denseT", [P, UNIT])
        held = sb("held", [P, NH, P])
        hot = sb("hot", [HOT_P, NH, 2, HOT_ROWS, D], F32R)
        onehot = [sb(f"onehot{i}", [HOT_P, HOT_ROWS, UNIT], F32R) for i in range(2)]
        row_of = sb("row_of", [HOT_P, HOT_ROWS])
        hot_idx = sb("hot_idx", [P, TILES, NH])
        hot_idxT = sb("hot_idxT", [P, B], F16)
        pick = sb("pick", [P, NH, P], F16)

        with nc.sbuf_tensor("stage", [HOT_P, STAGES, HOT_ROWS * D], F32) as stage:
            pass
        z = sb("z", [P, Q, UNIT])
        z_high = sb("z_high", [P, K1, UNIT], F32R)
        z_low = sb("z_low", [P, K1, UNIT], F32R)
        with nc.sbuf_tensor("wz", [P, K1, H1], F32) as wz:
            pass
        wz_low = sb("wz_low", [P, K1, H1], F32R)
        wz_high = sb("wz_high", [P, K1, H1], F32R)
        with nc.sbuf_tensor("w2s", [P, M1, H2], F32) as w2s:
            pass
        w2_low = sb("w2_low", [P, M1, H2], F32R)
        w2_high = sb("w2_high", [P, M1, H2], F32R)
        w3s = sb("w3s", [P, M2])
        b1s = sb("b1s", [P, M1])
        b2s = sb("b2s", [P, M2])
        with nc.sbuf_tensor("wd2", [P, H1], F32) as wd2, nc.sbuf_tensor("ones", [P, P], F32) as ones:
            pass
        h1_high = sb("h1_high", [P, M1, UNIT], F32R)
        h1_low = sb("h1_low", [P, M1, UNIT], F32R)
        h1 = sb("h1", [P, 2, UNIT])
        h2 = sb("h2", [P, M2, UNIT])
        y_sb = sb("y_sb", [P, TILES])

        t_ps = [ps(f"t_ps{i}", [P, 4, P]) for i in range(2)]
        g_ps = [ps(f"g_ps{i}", [P, 2, 512]) for i in range(2)]
        h_ps = ps("h_ps", [P, 512])
        s_ps = ps("s_ps", [P, 2, UNIT])

        idx_landed = sem("idx_landed")
        dense_landed = [sem(f"dense_landed{s}") for s in range(2)]
        gathered = [[sem(f"gathered{s}_{part}") for part in range(2)] for s in range(2)]
        table_landed = [sem(f"table_landed{s}") for s in range(STAGES)]
        w_landed = sem("w_landed")
        wd_landed = sem("wd_landed")
        bias_landed = sem("bias_landed")
        ones_set = sem("ones_set")
        ident_ready = sem("ident_ready")
        rows_numbered = sem("rows_numbered")
        idx_pad_zero = sem("idx_pad_zero")
        pads_zero = sem("pads_zero")
        hot_idxT_zero = sem("hot_idxT_zero")
        wz_zero = sem("wz_zero")
        wd_summed = sem("wd_summed")
        weights_high = sem("weights_high")
        weights_cut = sem("weights_cut")
        hot_idx_ready = sem("hot_idx_ready")
        hot_idx_turned = sem("hot_idx_turned")
        hot_idxT_ready = sem("hot_idxT_ready")
        pick_ready = sem("pick_ready")
        table_high = sem("table_high")
        table_cut = sem("table_cut")
        idx_copied = sem("idx_copied")
        parts_begun = sem("parts_begun")
        turned = sem("turned")
        spread = sem("spread")
        onehot_ready = sem("onehot_ready")
        looked_up = sem("looked_up")
        copied = [sem("copied_dve"), sem("copied_act")]
        held_moved = sem("held_moved")
        dense_high = sem("dense_high")
        dense_cut = sem("dense_cut")
        gram_done = sem("gram_done")
        z_dve = sem("z_dve")
        z_act = sem("z_act")
        z_high_cut = sem("z_high_cut")
        z_cut = sem("z_cut")
        h_done = sem("h_done")
        h_ready = sem("h_ready")
        h_low_cut = sem("h_low_cut")
        y_done = sem("y_done")
        y_copied = sem("y_copied")
        y_stored = sem("y_stored")

        block = ctx.enter_context(nc.Block())

        dense_tiles = dense.rearrange("(p t) d -> p t d", t=TILES)

        def weight_rows():
            out, row = [], D
            for f in range(COLS):
                for j in range(GROUP):
                    c0 = f + (j - f) % GROUP
                    n = -(-(COLS - c0) // GROUP)
                    if n > 0:
                        r0 = row + c0 - f
                        part = ROWS * j + f
                        out.append((wz[part:part + 1, c0 // GROUP:c0 // GROUP + n, :],
                                    w1[r0:r0 + GROUP * (n - 1) + 1:GROUP, :].rearrange("(o q) n -> o q n", o=1)))
                row += COLS - f
            return out

        LOADS = weight_rows()

        @block.sync
        def _(sp):
            sp.dma_start(idx[:, 0:TILES, :], ids.rearrange("(p t) f -> p t f", t=TILES)).then_inc(idx_landed, 16)

            def load_dense(t, slot):
                sp.dma_start(emb[:, slot, 0, :], dense_tiles[:, bass.ds(t, 1), :].rearrange("p o d -> p (o d)")
                             ).then_inc(dense_landed[slot], 16)

            def load_weights(n, of):
                for dst, src in LOADS[n::of]:
                    sp.dma_start(dst, src).then_inc(w_landed, 16)

            for h, f in enumerate(HOT):
                if h >= STAGES:
                    sp.wait_ge(table_cut, h - STAGES + 1)
                sp.dma_start(stage[:, h % STAGES, :], tables[f].rearrange("(p k) d -> p (k d)", k=HOT_ROWS)
                             ).then_inc(table_landed[h % STAGES], 16)
                if h == 1:
                    for slot in range(2):
                        load_dense(slot, slot)
            sp.wait_ge(wz_zero, 1)
            load_weights(0, 2)
            for slot in range(2):
                sp.wait_ge(turned, NCOLD[0] + slot * NCOLD[1])
                load_dense(2 + slot, slot)
                load_weights(1 + 2 * slot, 4)
            with sp.Fori(2, UNITS) as u:
                for slot in range(2):
                    sp.wait_ge(turned, TURNS * (u - 1) + NCOLD[0] + slot * NCOLD[1])
                    load_dense(2 * u + slot, slot)
            sp.wait_ge(y_copied, UNITS)
            sp.dma_start(y.rearrange("(p t) o -> p (t o)", t=TILES), y_sb[:]).then_inc(y_stored, 16)
            sp.wait_ge(y_stored, 16)

        @block.gpsimd
        def _(pool):
            pool.memset(ones[:], 1.0).then_inc(ones_set, 1)
            pool.wait_ge(ones_set, 1)
            pool.affine_select(out=ident[:], in_=ones[:], compare_op=ALU.is_equal, fill=0.0, base=0,
                               pattern=[[-1, P]], channel_multiplier=1).then_inc(ident_ready, 1)
            pool.iota(row_of[:], [[1, HOT_ROWS]], base=0, channel_multiplier=HOT_ROWS,
                      allow_small_or_imprecise_dtypes=True).then_inc(rows_numbered, 1)

            with pool.Fori(0, UNITS) as u:
                for slot in range(2):
                    for part in range(2):
                        pool.wait_ge(idx_copied, 4 * u + 2 * slot + part + 1)
                        pool.sem_inc(parts_begun, 1)
                        for f in GATHERS[part]:
                            pool.indirect_dma_start(
                                emb[:, slot, slot_of[f + 1], :], None, tables[f][:, :],
                                bass.IndirectOffsetOnAxis(ap=idx_slot[:, slot, f:f + 1], axis=0)
                            ).then_inc(gathered[slot][part], 16)

        @block.tensor
        def _(pe):
            def spread_indices(u, c):
                if not (is_first(u) and c == 0):
                    pe.wait_ge(onehot_ready, NH * u + 2 * c)
                for n in range(2):
                    last = pe.matmul(s_ps[:, n, :], pick[:, 2 * c + n, :], hot_idxT[:, bass.ds(UNIT * u, UNIT)],
                                     start=True, stop=True)
                last.then_inc(spread, 1)

            def look_up(u, c, bank):
                for n in range(2):
                    h = 2 * c + n
                    if is_first(u):
                        pe.wait_ge(table_cut, h + 1)
                    pe.wait_ge(onehot_ready, NH * u + h + 1)
                    if n == 1 and c + 1 < HOT_RUNS:
                        spread_indices(u, c + 1)
                    out = t_ps[bank][:, 2 * n:2 * n + 2, :].rearrange("d a s -> d (a s)")
                    for part in (1, 0):
                        for k in range(HOT_ROWS):
                            last = pe.matmul(out, hot[:, h, part, k, :], onehot[n][:, k, :],
                                             start=(part == 1 and k == 0), stop=(part == 0 and k == HOT_ROWS - 1))
                    last.then_inc(looked_up, 1)

            def turn(u, slot, run, bank):
                if run == 0:
                    pe.wait_ge(dense_landed[slot], 16 * (u + 1))
                if run in (0, FIRST):
                    part = run // FIRST
                    pe.wait_ge(gathered[slot][part], 16 * len(GATHERS[part]) * (u + 1))
                for n, f in enumerate(COLD_RUNS[slot][run]):
                    last = pe.transpose(t_ps[bank][:, n, :], emb[:, slot, slot_of[f], :], ident[:])
                last.then_inc(turned, 1)

            def fill(u, slot, kind, run):
                bank, _, _ = NUMBERED[is_first(u)][slot, kind, run]
                before = [k for k in NUMBERED[is_first(u)] if NUMBERED[is_first(u)][k][0] == bank]
                at = before.index((slot, kind, run))
                if at:
                    _, who, n = NUMBERED[is_first(u)][before[at - 1]]
                    pe.wait_ge(copied[who], COPIES[who] * u + n + 1)
                elif not is_first(u):
                    was = is_first(u - 1) if isinstance(u, int) else False
                    last = [k for k in NUMBERED[was] if NUMBERED[was][k][0] == bank][-1]
                    _, who, n = NUMBERED[was][last]
                    pe.wait_ge(copied[who], COPIES[who] * (u - 1) + n + 1)
                if kind == "hot":
                    look_up(u, run, bank)
                else:
                    turn(u, slot, run, bank)

            def gram(u, slot, i):
                m = 2 * GRAMS * u + GRAMS * slot + i // 2
                if i == 0:
                    for who in (DVE, SCALAR):
                        n = 1 + max(v[2] for k, v in NUMBERED[False].items() if k[0] <= slot and v[1] == who)
                        pe.wait_ge(copied[who], COPIES[who] * u + n)
                    if slot:
                        pe.wait_ge(held_moved, u + 1)
                if i % 2 == 0 and not (is_first(u) and slot == 0 and i < 4):
                    pe.wait_ge(z_dve, m - 1)
                    pe.wait_ge(z_act, m - 1)
                x = xT[:, slot]
                for n in range(IN_BANK):
                    s0 = GROUP * (IN_BANK * i + n)
                    last = pe.matmul(g_ps[i // 2 % 2][0:P - ROWS + FEATS, i % 2, n * WIDE:(n + 1) * WIDE],
                                     x[:, s0:s0 + GROUP, :].rearrange("d s f -> d (s f)")[:, 0:P - ROWS + FEATS],
                                     x[:, s0:s0 + GROUP, 1:FEATS], start=True, stop=True)
                if i % 2 == 1:
                    last.then_inc(gram_done, 1)

            def in_parts(out, w_high, w_low, x_high, x_low, start, stop):
                pe.matmul(out, w_low, x_high, start=start, stop=False)
                pe.matmul(out, w_high, x_low, start=False, stop=False)
                return pe.matmul(out, w_high, x_high, start=False, stop=stop)

            def layers(u, i):
                out = h_ps[:, 0:UNIT]
                if i < M1:
                    if i == 0:
                        if is_first(u):
                            pe.wait_ge(weights_cut, 2)
                            pe.wait_ge(bias_landed, 64)
                        else:
                            pe.wait_ge(y_copied, u)
                        pe.wait_ge(z_cut, 2 * (u + 1))
                        pe.wait_ge(dense_cut, u + 1)
                    else:
                        pe.wait_ge(h_ready, HUSES * u + i)
                    cols = slice(P * i, P * (i + 1))
                    for q in range(K1):
                        last = in_parts(out, wz_high[:, q, cols], wz_low[:, q, cols], z_high[:, q, :],
                                        z_low[:, q, :], q == 0, q == K1 - 1)
                    last.then_inc(h_done, 1)
                elif i < HUSES:
                    cols = slice(P * (i - M1), P * (i - M1 + 1))
                    pe.wait_ge(h_ready, HUSES * u + i)
                    if i == M1:
                        pe.wait_ge(h_low_cut, M1 * (u + 1))
                    for k in range(M1):
                        last = in_parts(out, w2_high[:, k, cols], w2_low[:, k, cols], h1_high[:, k, :],
                                        h1_low[:, k, :], k == 0, k == M1 - 1)
                    last.then_inc(h_done, 1)
                else:
                    pe.wait_ge(h_ready, HUSES * (u + 1))
                    for tile in range(2):
                        for c in range(M2):
                            last = pe.matmul(h_ps[:, tile:tile + 1], h2[:, c, P * tile:P * (tile + 1)],
                                             w3s[:, c:c + 1], start=(c == 0), stop=(c == M2 - 1))
                    last.then_inc(y_done, 1)

            def step(u, slot, new=True, grams=True, unit=True, ahead=True):
                for i in range(PIECES):
                    if new:
                        for kind, run in plan_of(u, slot)[i]:
                            fill(u, slot, kind, run)
                    if grams:
                        gram(u if slot else u - 1, 1 - slot, i)
                    if new and ahead and slot and i == 0:
                        spread_indices(u + 1, 0)
                    if slot and unit and i:
                        layers(u - 1, i - 1)

            pe.wait_ge(ident_ready, 1)
            pe.wait_ge(hot_idx_ready, 1)
            for t in range(TILES):
                c = t // 4
                last = pe.transpose(g_ps[c // 2][0:NH, c % 2, P * (t % 4):P * (t % 4 + 1)], hot_idx[:, t, :],
                                    ident[:])
            last.then_inc(hot_idx_turned, 1)
            pe.wait_ge(hot_idxT_ready, 1)
            pe.wait_ge(pick_ready, 1)
            spread_indices(0, 0)

            step(0, 0, grams=False)
            pe.wait_ge(pads_zero, 1)
            step(0, 1, unit=False)
            step(1, 0)
            step(1, 1)
            with pe.Fori(2, UNITS - 1) as u:
                step(u, 0)
                step(u, 1)
            step(UNITS - 1, 0)
            step(UNITS - 1, 1, ahead=False)
            step(UNITS, 0, new=False)
            step(UNITS, 1, new=False, grams=False)

        def copy_bank(engine, copy, u, slot, kind, run):
            bank, who, _ = NUMBERED[is_first(u)][slot, kind, run]
            if kind == "cold":
                engine.wait_ge(turned, TURNS * u + NCOLD[0] * slot + run + 1)
                runs = COLD_RUNS[slot][run]
                if run == 0:
                    if slot == 0 and not is_first(u):
                        engine.wait_ge(dense_cut, u)
                    copy(denseT[:, P * slot:P * (slot + 1)], t_ps[bank][:, 0, :])
                copy(xT[:, slot, :, runs[0]:runs[-1] + 1].rearrange("d s f -> d f s"),
                     t_ps[bank][:, 0:len(runs), :]).then_inc(copied[who], 1)
            else:
                engine.wait_ge(looked_up, NH * u + 2 * run + 2)
                f0, f1 = HOT[2 * run] + 1, HOT[2 * run + 1] + 1
                both = t_ps[bank][:].rearrange("d (h a) s -> d h a s", h=2)
                copy(xT[:, 0, :, f0:f1 + 1:f1 - f0].rearrange("d s f -> d f s"), both[:, :, 0, :])
                copy(held[:, 2 * run:2 * run + 2, :], both[:, :, 1, :]).then_inc(copied[who], 1)

        def copy_pairs(engine, copy, u, slot, m, members, done):
            engine.wait_ge(gram_done, 2 * GRAMS * u + GRAMS * slot + m + 1)
            g = g_ps[m % 2][:, :, 0:IN_BANK * WIDE].rearrange("r e (n s c) -> r e n s c", n=IN_BANK, s=GROUP)
            size = 2 * GROUP * IN_BANK
            s0 = P * slot + size * m
            zz = z[:, :, s0:s0 + size].rearrange("r q (e n s) -> r s e n q", e=2, s=GROUP)
            for s in members:
                for j in range(GROUP):
                    nq = -(-(COLS - j) // GROUP)
                    last = copy(zz[ROWS * j:ROWS * j + FEATS, s, :, :, 0:nq],
                                g[ROWS * s:ROWS * s + FEATS, :, :, s, j:j + GROUP * (nq - 1) + 1:GROUP])
            last.then_inc(done, 1)

        @block.vector
        def _(dve):
            dve.memset(idx[:, TILES:, :], 0).then_inc(idx_pad_zero, 1)
            dve.wait_ge(idx_landed, 16)
            for slot in range(2):
                for part in range(2):
                    dve.tensor_copy(idx_slot[:, slot, SPAN[part]], idx[:, slot, SPAN[part]]).then_inc(idx_copied, 1)
            for h, f in enumerate(HOT):
                last = dve.tensor_copy(hot_idx[:, :, h], idx[:, 0:TILES, f])
            last.then_inc(hot_idx_ready, 1)
            dve.memset(hot_idxT[:], 0.0).then_inc(hot_idxT_zero, 1)
            dve.wait_ge(ident_ready, 1)
            for h in range(NH):
                last = dve.tensor_copy(pick[:, h, :], ident[:, h:h + 1].to_broadcast([P, P]))
            last.then_inc(pick_ready, 1)
            dve.memset(wz[:], 0.0).then_inc(wz_zero, 1)

            def one_hot(u, h):
                dve.wait_ge(spread, HOT_RUNS * u + h // 2 + 1)
                if not (is_first(u) and h < 2):
                    dve.wait_ge(looked_up, NH * u + h - 1)
                here = s_ps[0:HOT_P, h % 2, :].unsqueeze(1).to_broadcast([HOT_P, HOT_ROWS, UNIT])
                rows = row_of[:].unsqueeze(2).to_broadcast([HOT_P, HOT_ROWS, UNIT])
                dve.tensor_tensor(onehot[h % 2][:], here, rows, ALU.is_equal).then_inc(onehot_ready, 1)

            def cut_table(h):
                dve.wait_ge(table_high, h + 1)
                part = hot[:, h].rearrange("p a k d -> p a (k d)")
                dve.tensor_tensor(part[:, 1, :], stage[:, h % STAGES, :], part[:, 0, :].bitcast(F32),
                                  ALU.subtract).then_inc(table_cut, 1)

            def cut_dense(u):
                dve.wait_ge(dense_high, u + 1)
                dve.tensor_tensor(z_low[:, Q, :], denseT[:], z_high[:, Q, :].bitcast(F32),
                                  ALU.subtract).then_inc(dense_cut, 1)

            def cut_z(u, tile):
                cols = slice(P * tile, P * (tile + 1))
                dve.wait_ge(z_high_cut, 2 * u + tile + 1)
                dve.tensor_tensor(z_low[:, 0:Q, cols], z[:, :, cols], z_high[:, 0:Q, cols].bitcast(F32),
                                  ALU.subtract).then_inc(z_cut, 1)

            def step(u, slot, new=True, grams=True, unit=True, ahead=True):
                if slot == 0 and not is_first(u):
                    cut_dense(u - 1)
                    cut_z(u - 1, 0)
                if slot and unit:
                    cut_z(u - 1, 1)
                for i in range(PIECES):
                    if new:
                        for kind, run in plan_of(u, slot)[i]:
                            if kind == "hot" and run + 1 < HOT_RUNS:
                                one_hot(u, 2 * run + 2)
                                if is_first(u):
                                    one_hot(u, 2 * run + 3)
                        if i and slot == 0 and not is_first(u):
                            for kind, run in plan_of(u, slot)[i - 1]:
                                if kind == "hot" and run + 1 < HOT_RUNS:
                                    one_hot(u, 2 * run + 3)
                        for kind, run in plan_of(u, slot)[i]:
                            if engine_of(kind, run) == DVE:
                                copy_bank(dve, dve.tensor_copy, u, slot, kind, run)
                    if grams and i % 2 == 1:
                        copy_pairs(dve, dve.tensor_copy, u if slot else u - 1, 1 - slot, i // 2, (0, 1), z_dve)
                    if new and i in (FIRST - 1, NCOLD[slot] - 1):
                        part = int(i >= FIRST)
                        dve.wait_ge(turned, TURNS * u + NCOLD[0] * slot + i + 1)
                        dve.tensor_copy(idx_slot[:, slot, SPAN[part]], idx[:, bass.ds(2 * u + slot + 2, 1), SPAN[part]]
                                        .rearrange("p o f -> p (o f)")).then_inc(idx_copied, 1)
                    if slot and unit and 0 < i <= M1:
                        c = i - 1
                        dve.wait_ge(h_ready, HUSES * (u - 1) + c + 1)
                        dve.tensor_tensor(h1_low[:, c, :], h1[:, c % 2, :], h1_high[:, c, :].bitcast(F32),
                                          ALU.subtract).then_inc(h_low_cut, 1)
                    if new and ahead and slot and i in (2, 4):
                        one_hot(u + 1, i // 2 - 1)

            dve.wait_ge(rows_numbered, 1)
            cut_table(0)
            one_hot(0, 0)
            cut_table(1)
            one_hot(0, 1)
            for h in range(2, NH):
                cut_table(h)
            dve.wait_ge(idx_pad_zero, 1)
            dve.memset(xT[:, :, :, FEATS:ROWS], 0.0)
            dve.wait_ge(table_cut, NH)
            dve.memset(z[:], 0.0).then_inc(pads_zero, 1)

            step(0, 0, grams=False)
            dve.wait_ge(pads_zero, 1)
            step(0, 1, unit=False)
            dve.wait_ge(wd_landed, 32)
            dve.tensor_tensor(wz[:, Q, :], wz[:, Q, :], wd2[:], ALU.add).then_inc(wd_summed, 1)
            step(1, 0)
            dve.wait_ge(weights_high, 2)
            dve.tensor_tensor(wz_low[:], wz[:], wz_high[:].bitcast(F32), ALU.subtract).then_inc(weights_cut, 1)
            dve.tensor_tensor(w2_low[:], w2s[:], w2_high[:].bitcast(F32), ALU.subtract).then_inc(weights_cut, 1)
            step(1, 1)
            with dve.Fori(2, UNITS - 1) as u:
                step(u, 0)
                step(u, 1)
            step(UNITS - 1, 0)
            step(UNITS - 1, 1, ahead=False)
            step(UNITS, 0, new=False)
            step(UNITS, 1, new=False, grams=False)

        @block.scalar
        def _(act):
            act.dma_start(w2s[:], w2.rearrange("(m p) n -> p m n", p=P)).then_inc(bias_landed, 16)
            with nc.allow_non_contiguous_dma(reason="a few hundred words, once"):
                act.dma_start(b1s[:], b1.rearrange("(m p) -> p m", p=P)).then_inc(bias_landed, 16)
                act.dma_start(b2s[:], b2.rearrange("(m p) -> p m", p=P)).then_inc(bias_landed, 16)
                act.dma_start(w3s[:], w3.rearrange("(m p) o -> p (m o)", p=P)).then_inc(bias_landed, 16)
            act.dma_start(wd2[:], w1[D + PAIRS:2 * D + PAIRS, :]).then_inc(wd_landed, 16)

            def table_part(h):
                act.wait_ge(table_landed[h % STAGES], 16 * (h // STAGES + 1))
                act.copy(hot[:, h, 0].rearrange("p k d -> p (k d)"), stage[:, h % STAGES, :]).then_inc(table_high, 1)

            act.wait_ge(hot_idxT_zero, 1)
            act.wait_ge(hot_idx_turned, 1)
            for c in range(4):
                last = act.copy(hot_idxT[0:NH, 512 * c:512 * (c + 1)], g_ps[c // 2][0:NH, c % 2, :])
            last.then_inc(hot_idxT_ready, 1)
            for h in range(NH):
                table_part(h)
            act.wait_ge(wz_zero, 1)
            act.dma_start(wz[:, Q, :], w1[0:D, :]).then_inc(wd_landed, 16)

            def cut_dense(u):
                if not is_first(u):
                    act.wait_ge(h_done, HUSES * (u - 1) + M1)
                act.wait_ge(copied[DVE], COPIES[DVE] * u + NUMBERED[False][1, "cold", 0][2] + 1)
                act.copy(z_high[:, Q, :], denseT[:]).then_inc(dense_high, 1)

            def cut_z(u, tile):
                act.wait_ge(z_dve, GRAMS * (2 * u + tile + 1))
                act.wait_ge(z_act, GRAMS * (2 * u + tile + 1))
                cols = slice(P * tile, P * (tile + 1))
                act.copy(z_high[:, 0:Q, cols], z[:, :, cols]).then_inc(z_high_cut, 1)

            def move_held(u):
                act.wait_ge(copied[SCALAR], COPIES[SCALAR] * u + 1 + max(
                    v[2] for k, v in NUMBERED[is_first(u)].items() if k[1] == "hot"))
                h = 0
                while h < NH:
                    n = 1
                    while h + n < NH and HOT[h + n] == HOT[h] + n:
                        n += 1
                    f0 = HOT[h] + 1
                    last = act.copy(xT[:, 1, :, f0:f0 + n].rearrange("d s f -> d f s"), held[:, h:h + n, :])
                    h += n
                last.then_inc(held_moved, 1)

            def layers(u, i):
                if i < HUSES:
                    act.wait_ge(h_done, HUSES * u + i + 1)
                    if i < M1:
                        if not (is_first(u) and i < 2):
                            act.wait_ge(h_low_cut, M1 * u + i - 1)
                        act.activation(h1_high[:, i, :], h_ps[:, 0:UNIT], ACT.Relu, bias=b1s[:, i:i + 1])
                        act.activation(h1[:, i % 2, :], h_ps[:, 0:UNIT], ACT.Relu,
                                       bias=b1s[:, i:i + 1]).then_inc(h_ready, 1)
                    else:
                        act.activation(h2[:, i - M1, :], h_ps[:, 0:UNIT], ACT.Relu,
                                       bias=b2s[:, i - M1:i - M1 + 1]).then_inc(h_ready, 1)
                else:
                    act.wait_ge(y_done, u + 1)
                    act.copy(y_sb[:, bass.ds(2 * u, 2)], h_ps[:, 0:2]).then_inc(y_copied, 1)

            def step(u, slot, new=True, grams=True, unit=True):
                if slot == 0 and not is_first(u):
                    cut_dense(u - 1)
                    cut_z(u - 1, 0)
                if slot and unit:
                    cut_z(u - 1, 1)
                if slot and new:
                    move_held(u)
                for i in range(PIECES):
                    if new:
                        for kind, run in plan_of(u, slot)[i]:
                            if engine_of(kind, run) == SCALAR:
                                copy_bank(act, act.copy, u, slot, kind, run)
                    if grams and i % 2 == 1:
                        if i == 1 and not is_first(u) and not (slot == 0 and isinstance(u, int) and u == 1):
                            act.wait_ge(z_cut, 2 * u - 1 if slot else 2 * u - 2)
                        copy_pairs(act, act.copy, u if slot else u - 1, 1 - slot, i // 2, (2, 3), z_act)
                    if slot and unit and i:
                        layers(u - 1, i - 1)

            step(0, 0, grams=False)
            act.wait_ge(pads_zero, 1)
            step(0, 1, unit=False)
            step(1, 0)
            act.wait_ge(w_landed, 16 * len(LOADS))
            act.wait_ge(wd_summed, 1)
            act.copy(wz_high[:], wz[:]).then_inc(weights_high, 1)
            act.wait_ge(bias_landed, 64)
            act.copy(w2_high[:], w2s[:]).then_inc(weights_high, 1)
            step(1, 1)
            with act.Fori(2, UNITS - 1) as u:
                step(u, 0)
                step(u, 1)
            step(UNITS - 1, 0)
            step(UNITS - 1, 1)
            step(UNITS, 0, new=False)
            step(UNITS, 1, new=False, grams=False)


def kernel(**inputs):
    import numpy as _np
    import concourse.bacc as _bacc
    from concourse import mybir as _mybir
    from concourse.bass_utils import run_bass_kernel_spmd as _run

    nc = _bacc.Bacc("TRN2", target_bir_lowering=False, num_devices=1)
    arrays, aps = {}, {}
    for name, value in inputs.items():
        a = _np.ascontiguousarray(value)
        arrays[f"in_{name}"] = a
        aps[name] = nc.dram_tensor(f"in_{name}", a.shape, _mybir.dt.from_np(a.dtype), kind="ExternalInput").ap()
    n_tables = aps["ids"].shape[1]
    y = nc.dram_tensor("out_y", (aps["ids"].shape[0], 1), _mybir.dt.float32, kind="ExternalOutput").ap()
    dlrm_tower(nc, aps["r_dense_features"], aps["ids"], [aps[f"tbl_{f}"] for f in range(n_tables)],
               aps["W_top1"], aps["b_top1"], aps["W_top2"], aps["b_top2"], aps["W_top3"], y)
    r = _run(nc, [arrays], core_ids=[0])
    return r.results[0]["out_y"]
```

```python
from contextlib import ExitStack

import concourse.bass as bass
from concourse import mybir

F32 = mybir.dt.float32
F32R = mybir.dt.float32r
F16 = mybir.dt.float16
I32 = mybir.dt.int32
ALU = mybir.AluOpType
ACT = mybir.ActivationFunctionType

P = 128
HOT_TABLE = 1000
HOT_ROWS = 8
MAX_HOT = 7


def dlrm_tower(nc, dense, ids, tables, w1, b1, w2, b2, w3, y):
    B, D = dense.shape
    NF = len(tables)
    FEATS = NF + 1
    PAIRS = FEATS * NF // 2
    H1, H2 = w2.shape
    TILES = B // P
    UNITS = TILES // 2
    UNIT = 2 * P
    M1, M2 = H1 // P, H2 // P
    CHUNKS = M1 + M2
    assert D == P and w1.shape[0] == 2 * D + PAIRS and TILES == 2 * UNITS and UNITS % 2 == 0

    HOT = []
    for f in reversed(range(NF - 1)):
        if len(HOT) < MAX_HOT and f + 1 not in HOT and tables[f].shape[0] == tables[f + 1].shape[0] == HOT_TABLE:
            HOT = [f, f + 1] + HOT if len(HOT) + 1 < MAX_HOT else HOT + [f + 1]
    COLD = [f for f in range(NF) if f not in HOT]
    NH, NC = len(HOT), len(COLD)
    HOT_P = HOT_TABLE // HOT_ROWS
    HOT_RUN = [range(h, min(h + 2, NH)) for h in range(0, NH, 2)]
    HOT_RUNS = len(HOT_RUN)
    STAGES = 5
    assert HOT_P <= P

    turned_features = [0] + [f + 1 for f in COLD]
    slot_of = {f: n for n, f in enumerate(turned_features)}
    cold = []
    for f in turned_features:
        if cold and len(cold[-1]) < 4 and cold[-1][-1] == f - 1:
            cold[-1].append(f)
        else:
            cold.append([f])
    COLD_RUNS = [cold, cold[:-1] + [cold[-1][:1], cold[-1][1:]] if HOT_RUNS % 2 else cold]
    NCOLD = [len(runs) for runs in COLD_RUNS]
    TURNS = sum(NCOLD)
    FIRST = (NCOLD[0] + 1) // 2
    GATHERS = [[f - 1 for run in cold[:FIRST] for f in run if f], [f - 1 for run in cold[FIRST:] for f in run]]
    assert len(cold[-1]) > 1 and (TURNS + HOT_RUNS) % 2 == 0

    SPAN = [slice(fields[0], fields[-1] + 1) for fields in GATHERS]

    PIECES = 8
    assert max(NCOLD) <= PIECES

    def places(first, per, n):
        return [(first + k * PIECES // per, k) for k in range(n)]

    def plan(cold_at, hot_at):
        out = [[] for _ in range(PIECES)]
        for kind, at in (("hot", hot_at), ("cold", cold_at)):
            for piece, run in at:
                out[piece].append((kind, run))
        return out

    early = [places(0, PIECES, n) for n in NCOLD]
    spread_out = early[0][:-1] + [(5, NCOLD[0] - 1)]

    def waiting(early_runs, n, piece):
        return [(piece + run if run < early_runs else PIECES - 1, run) for run in range(n)]

    START, MIDDLE, END = [
        [plan(early[0], [(0, 0), (0, 1)] + [(FIRST + 2 * n, 2 + n) for n in range(HOT_RUNS - 2)]),
         plan(places(2, PIECES, NCOLD[1]), [(2 * n + (n == 0), n) for n in range(HOT_RUNS)])],
        [plan(spread_out, []), plan(early[1], places(0, HOT_RUNS, HOT_RUNS))],
        [plan(waiting(FIRST, NCOLD[0], 0), []), plan(waiting(FIRST, NCOLD[1], 3), [])]]

    END_LAYERS = [{PIECES - 1: range(M1)}, {0: range(M1, CHUNKS), 1: [CHUNKS]}]

    def is_first(u):
        return isinstance(u, int) and u == 0

    def plans_of(u):
        return START if is_first(u) else END if isinstance(u, int) and u == UNITS - 1 else MIDDLE

    BANKS = TURNS + HOT_RUNS

    def numbers(u, slot, kinds=("cold", "hot")):
        at, out = 0, {}
        for s, pieces in enumerate(plans_of(u)):
            for kind, run in [bank for piece in pieces for bank in piece]:
                if s == slot and kind in kinds:
                    out[kind, run] = (0, at) if is_first(u) else (BANKS, HOT_RUNS + at)
                at += 1
        return out

    def number(u, slot, kind, run):
        per_unit, offset = numbers(u, slot)[kind, run]
        return per_unit * u + offset

    def last_number(u, slot, kind):
        per_unit, offset = max(numbers(u, slot, (kind,)).values())
        return per_unit * u + offset

    def parity_of(u, slot, kind, run):
        return numbers(u, slot)[kind, run][1] % 2

    ROWS = 32
    GROUP = P // ROWS
    IN_BANK = 4
    GRAMS = 4
    COLS = FEATS - 1
    WIDE = GROUP * COLS
    Q = -(-COLS // GROUP)
    PQ = -(-PAIRS // P)
    K1 = PQ + 1
    assert K1 + M1 <= PIECES and GRAMS * 2 * IN_BANK * GROUP == P and ROWS >= FEATS and IN_BANK * WIDE <= 512

    with ExitStack() as ctx:
        def sb(name, shape, dt=F32):
            return ctx.enter_context(nc.sbuf_tensor(name, shape, dt))

        def ps(name, shape, dt=F32):
            return ctx.enter_context(nc.psum_tensor(name, shape, dt))

        def sem(name):
            return ctx.enter_context(nc.semaphore(name))

        idx = sb("idx", [P, TILES + 2, NF], I32)
        idx_slot = sb("idx_slot", [P, 2, NF], I32)
        emb = sb("emb", [P, 2, NC + 1, D])
        ident = sb("ident", [P, P])
        xT = sb("xT", [P, 2, P, ROWS])
        denseT = [sb(f"denseT{i}", [P, UNIT]) for i in range(2)]
        held = sb("held", [P, 2, NH, P])
        hot = sb("hot", [HOT_P, NH, 2, HOT_ROWS, D], F32R)
        onehot = [sb(f"onehot{i}", [HOT_P, HOT_ROWS, UNIT], F32R) for i in range(2)]
        row_of = sb("row_of", [HOT_P, HOT_ROWS])
        hot_idx = sb("hot_idx", [P, TILES, NH])
        hot_idxT = sb("hot_idxT", [P, B], F16)
        pick = sb("pick", [P, NH, P], F16)

        with nc.sbuf_tensor("stage", [HOT_P, STAGES, HOT_ROWS * D], F32) as stage:
            pass
        z = [sb(f"z{i}", [P, Q, UNIT]) for i in range(2)]
        z_pack = sb("z_pack", [P, PQ, UNIT])
        z_high = sb("z_high", [P, K1, UNIT], F32R)
        z_low = sb("z_low", [P, K1, UNIT], F32R)
        with nc.sbuf_tensor("wz", [P, K1, H1], F32) as wz:
            pass
        wz_low = sb("wz_low", [P, K1, H1], F32R)
        wz_high = sb("wz_high", [P, K1, H1], F32R)
        with nc.sbuf_tensor("w2s", [P, M1, H2], F32) as w2s:
            pass
        w2_low = sb("w2_low", [P, M1, H2], F32R)
        w2_high = sb("w2_high", [P, M1, H2], F32R)
        w3s = sb("w3s", [P, M2])
        b1s = sb("b1s", [P, M1])
        b2s = sb("b2s", [P, M2])
        with nc.sbuf_tensor("wd2", [P, H1], F32) as wd2, nc.sbuf_tensor("ones", [P, P], F32) as ones:
            pass
        h1_high = sb("h1_high", [P, M1, UNIT], F32R)
        h1_low = sb("h1_low", [P, M1, UNIT], F32R)
        h1 = sb("h1", [P, 2, UNIT])
        h2 = sb("h2", [P, M2, UNIT])
        y_sb = sb("y_sb", [P, TILES])

        t_ps = [ps(f"t_ps{i}", [P, 4, P]) for i in range(2)]
        g_ps = [ps(f"g_ps{i}", [P, 2, 512]) for i in range(2)]
        h_ps = ps("h_ps", [P, 512])
        s_ps = ps("s_ps", [P, 2, UNIT])

        idx_landed = sem("idx_landed")
        dense_landed = [sem(f"dense_landed{s}") for s in range(2)]
        gathered = [[sem(f"gathered{s}_{part}") for part in range(2)] for s in range(2)]
        table_landed = [sem(f"table_landed{s}") for s in range(STAGES)]
        w1_landed = sem("w1_landed")
        small_landed = sem("small_landed")
        ones_set = sem("ones_set")
        ident_ready = sem("ident_ready")
        rows_numbered = sem("rows_numbered")
        idx_pad_zero = sem("idx_pad_zero")
        pads_zero = sem("pads_zero")
        hot_idxT_zero = sem("hot_idxT_zero")
        wz_zero = sem("wz_zero")
        wd_summed = sem("wd_summed")
        weights_high = sem("weights_high")
        weights_cut = sem("weights_cut")
        hot_idx_ready = sem("hot_idx_ready")
        hot_idx_turned = sem("hot_idx_turned")
        hot_idxT_ready = sem("hot_idxT_ready")
        pick_ready = sem("pick_ready")
        table_high = sem("table_high")
        table_cut = sem("table_cut")
        idx_copied = sem("idx_copied")
        parts_begun = sem("parts_begun")
        sp_waited = sem("sp_waited")
        turned = sem("turned")
        spread = sem("spread")
        onehot_ready = sem("onehot_ready")
        looked_up = sem("looked_up")
        copied = sem("copied")
        held_moved = sem("held_moved")
        dense_high = sem("dense_high")
        dense_cut = sem("dense_cut")
        gram_done = sem("gram_done")
        z_dve = sem("z_dve")
        z_act = sem("z_act")
        z_packed = sem("z_packed")
        last_packed_sp = [sem(f"last_packed_sp{q}") for q in range(PQ)]
        last_packed_pool = [sem(f"last_packed_pool{q}") for q in range(PQ)]
        z_high_cut = sem("z_high_cut")
        z_cut = sem("z_cut")
        h_done = sem("h_done")
        h_ready = sem("h_ready")
        h_low_cut = sem("h_low_cut")
        y_done = sem("y_done")
        y_copied = sem("y_copied")
        y_stored = sem("y_stored")

        block = ctx.enter_context(nc.Block())

        dense_tiles = dense.rearrange("(p t) d -> p t d", t=TILES)

        PACK, row = [], 0
        for f in range(COLS):
            r0 = row
            while r0 < row + COLS - f:
                r1 = min(row + COLS - f, (r0 // P + 1) * P)
                PACK.append((r0 // P, r0 % P, r0 % P + r1 - r0, f, f + 1 + r0 - row))
                r0 = r1
            row += COLS - f

        last_pack = emb[:, 0, 0:2 * PQ, :].rearrange("p (q t) d -> p q (t d)", q=PQ)

        POOL_PACK = [run for n, run in enumerate(PACK) if n % 5 in (2, 4)]
        SP_PACK = [run for run in PACK if run not in POOL_PACK]

        def pack_run(engine, run, parity, out):
            chunk, r0, r1, f, g = run
            part = ROWS * (f % GROUP) + g
            return engine.dma_start(out[r0:r1, chunk, :], z[parity][part:part + r1 - r0, f // GROUP, :])

        def weight_chunk(i):
            if i < K1:
                return wz_high[:, i, :], wz_low[:, i, :], wz[:, i, :]
            return w2_high[:, i - K1, :], w2_low[:, i - K1, :], w2s[:, i - K1, :]

        def layer_bank(i, two_banks):
            return s_ps[:, 0, :] if two_banks and i % 2 else h_ps[:, 0:UNIT]

        def last_bank(i):
            return g_ps[i // 2][:, i % 2, 0:UNIT]

        @block.sync
        def _(sp):
            sp.dma_start(idx[:, 0:TILES, :], ids.rearrange("(p t) f -> p t f", t=TILES)).then_inc(idx_landed, 16)

            def load_dense(t, slot):
                sp.dma_start(emb[:, slot, 0, :], dense_tiles[:, bass.ds(t, 1), :].rearrange("p o d -> p (o d)")
                             ).then_inc(dense_landed[slot], 16)

            def load_next_dense(u, slot):
                sp.wait_ge(turned, TURNS * u + NCOLD[0] * slot + 1)
                sp.sem_inc(sp_waited, 1)
                load_dense(2 * u + 2 + slot, slot)

            def pack(u, parity):
                sp.wait_ge(z_dve, 2 * GRAMS * (u + 1))
                sp.sem_inc(sp_waited, 1)
                sp.wait_ge(z_act, 2 * GRAMS * (u + 1))
                sp.sem_inc(sp_waited, 1)
                if not is_first(u):
                    sp.wait_ge(z_cut, u)
                    sp.sem_inc(sp_waited, 1)
                for run in PACK:
                    pack_run(sp, run, parity, z_pack).then_inc(z_packed, 16)

            for h, f in enumerate(HOT):
                if h >= STAGES:
                    sp.wait_ge(table_cut, h - STAGES + 1)
                sp.dma_start(stage[:, h % STAGES, :], tables[f].rearrange("(p k) d -> p (k d)", k=HOT_ROWS)
                             ).then_inc(table_landed[h % STAGES], 16)
                if h == 1:
                    for slot in range(2):
                        load_dense(slot, slot)
            load_next_dense(0, 0)
            load_next_dense(0, 1)
            load_next_dense(1, 0)
            sp.wait_ge(pads_zero, 1)
            pack(0, 0)
            load_next_dense(1, 1)
            with sp.Fori(1, UNITS // 2 - 1) as v:
                for parity in range(2):
                    load_next_dense(2 * v + parity, 0)
                    pack(2 * v + parity - 1, 1 - parity)
                    load_next_dense(2 * v + parity, 1)
            load_next_dense(UNITS - 2, 0)
            pack(UNITS - 3, 1)
            load_next_dense(UNITS - 2, 1)
            pack(UNITS - 2, 0)
            sp.wait_ge(z_dve, 2 * GRAMS * UNITS)
            sp.wait_ge(z_act, 2 * GRAMS * UNITS)
            for run in SP_PACK:
                pack_run(sp, run, 1, last_pack).then_inc(last_packed_sp[run[0]], 16)
            sp.wait_ge(y_copied, UNITS + 1)
            sp.dma_start(y.rearrange("(p t) o -> p (t o)", t=TILES), y_sb[:]).then_inc(y_stored, 16)
            sp.wait_ge(y_stored, 16)

        @block.gpsimd
        def _(pool):
            pool.memset(ones[:], 1.0).then_inc(ones_set, 1)
            pool.wait_ge(ones_set, 1)
            pool.affine_select(out=ident[:], in_=ones[:], compare_op=ALU.is_equal, fill=0.0, base=0,
                               pattern=[[-1, P]], channel_multiplier=1).then_inc(ident_ready, 1)
            pool.iota(row_of[:], [[1, HOT_ROWS]], base=0, channel_multiplier=HOT_ROWS,
                      allow_small_or_imprecise_dtypes=True).then_inc(rows_numbered, 1)

            with pool.Fori(0, UNITS) as u:
                for slot in range(2):
                    for part in range(2):
                        pool.wait_ge(idx_copied, 4 * u + 2 * slot + part + 1)
                        pool.sem_inc(parts_begun, 1)
                        for f in GATHERS[part]:
                            pool.indirect_dma_start(
                                emb[:, slot, slot_of[f + 1], :], None, tables[f][:, :],
                                bass.IndirectOffsetOnAxis(ap=idx_slot[:, slot, f:f + 1], axis=0)
                            ).then_inc(gathered[slot][part], 16)
            pool.wait_ge(z_dve, 2 * GRAMS * UNITS)
            pool.wait_ge(z_act, 2 * GRAMS * UNITS)
            for run in POOL_PACK:
                pack_run(pool, run, 1, last_pack).then_inc(last_packed_pool[run[0]], 16)

        @block.tensor
        def _(pe):
            def spread_indices(u, c):
                if not (is_first(u) and c == 0):
                    pe.wait_ge(onehot_ready, NH * u + 2 * c)
                for n, h in enumerate(HOT_RUN[c]):
                    last = pe.matmul(s_ps[:, n, :], pick[:, h, :], hot_idxT[:, bass.ds(UNIT * u, UNIT)],
                                     start=True, stop=True)
                last.then_inc(spread, 1)

            def look_up(u, c, bank):
                for n, h in enumerate(HOT_RUN[c]):
                    if is_first(u):
                        pe.wait_ge(table_cut, h + 1)
                    pe.wait_ge(onehot_ready, NH * u + h + 1)
                    if h == HOT_RUN[c][-1] and c + 1 < HOT_RUNS:
                        spread_indices(u, c + 1)
                    out = t_ps[bank][:, 2 * n:2 * n + 2, :].rearrange("d a s -> d (a s)")
                    for part in (1, 0):
                        for k in range(HOT_ROWS):
                            last = pe.matmul(out, hot[:, h, part, k, :], onehot[n][:, k, :],
                                             start=(part == 1 and k == 0), stop=(part == 0 and k == HOT_ROWS - 1))
                    last.then_inc(looked_up, 1)

            def turn(u, slot, run, bank):
                if run == 0:
                    pe.wait_ge(dense_landed[slot], 16 * (u + 1))
                if run in (0, FIRST):
                    part = run // FIRST
                    pe.wait_ge(gathered[slot][part], 16 * len(GATHERS[part]) * (u + 1))
                for n, f in enumerate(COLD_RUNS[slot][run]):
                    last = pe.transpose(t_ps[bank][:, n, :], emb[:, slot, slot_of[f], :], ident[:])
                last.then_inc(turned, 1)

            def fill(u, slot, kind, run):
                if not (is_first(u) and number(u, slot, kind, run) < 2):
                    pe.wait_ge(copied, number(u, slot, kind, run) - 1)
                if kind == "hot":
                    look_up(u + slot, run, parity_of(u, slot, kind, run))
                else:
                    turn(u, slot, run, parity_of(u, slot, kind, run))

            def gram(u, slot, i):
                m = 2 * GRAMS * u + GRAMS * slot + i // 2
                if i == 0:
                    pe.wait_ge(copied, last_number(u, slot, "cold") + 1)
                    pe.wait_ge(held_moved, 2 * u + slot + 1)
                if i % 2 == 0 and not (is_first(u) and slot == 0 and i < 4):
                    pe.wait_ge(z_dve, m - 1)
                    pe.wait_ge(z_act, m - 1)
                x = xT[:, slot]
                for n in range(IN_BANK):
                    s0 = GROUP * (IN_BANK * i + n)
                    last = pe.matmul(g_ps[i // 2 % 2][0:P - ROWS + FEATS, i % 2, n * WIDE:(n + 1) * WIDE],
                                     x[:, s0:s0 + GROUP, :].rearrange("d s f -> d (s f)")[:, 0:P - ROWS + FEATS],
                                     x[:, s0:s0 + GROUP, 0:COLS], start=True, stop=True)
                if i % 2 == 1:
                    last.then_inc(gram_done, 1)

            def in_parts(out, w_high, w_low, x_high, x_low, start, stop):
                pe.matmul(out, w_low, x_high, start=start, stop=False)
                pe.matmul(out, w_high, x_low, start=False, stop=False)
                return pe.matmul(out, w_high, x_high, start=False, stop=stop)

            def layers(u, i, two_banks=False):
                out = layer_bank(i, two_banks)
                if i == 0:
                    pe.wait_ge(y_copied, u + 1)
                    pe.wait_ge(z_cut, u + 1)
                    pe.wait_ge(dense_cut, u + 1)
                elif not two_banks or i == CHUNKS:
                    pe.wait_ge(h_ready, CHUNKS * u + i)
                elif i > 1:
                    pe.wait_ge(h_ready, CHUNKS * u + i - 1)
                if i < M1:
                    cols = slice(P * i, P * (i + 1))
                    for q in range(K1):
                        rows = PAIRS - P * q if q == PQ - 1 else P
                        last = in_parts(out, wz_high[0:rows, q, cols], wz_low[0:rows, q, cols],
                                        z_high[0:rows, q, :], z_low[0:rows, q, :], q == 0, q == K1 - 1)
                    last.then_inc(h_done, 1)
                elif i < CHUNKS:
                    cols = slice(P * (i - M1), P * (i - M1 + 1))
                    for k in range(M1):
                        if i == M1:
                            pe.wait_ge(h_ready, CHUNKS * u + k + 1)
                            pe.wait_ge(h_low_cut, M1 * u + k + 3)
                        last = in_parts(out, w2_high[:, k, cols], w2_low[:, k, cols], h1_high[:, k, :],
                                        h1_low[:, k, :], k == 0, k == M1 - 1)
                    last.then_inc(h_done, 1)
                else:
                    for tile in range(2):
                        for c in range(M2):
                            last = pe.matmul(h_ps[:, tile:tile + 1], h2[:, c, P * tile:P * (tile + 1)],
                                             w3s[:, c:c + 1], start=(c == 0), stop=(c == M2 - 1))
                    last.then_inc(y_done, 1)

            def last_first_layer():
                pe.wait_ge(z_dve, 2 * GRAMS * UNITS)
                pe.wait_ge(z_act, 2 * GRAMS * UNITS)
                for n, q in enumerate([PQ, *range(PQ)]):
                    if q == PQ:
                        pe.wait_ge(dense_cut, UNITS)
                    else:
                        pe.wait_ge(z_cut, UNITS + q)
                    rows = PAIRS - P * q if q == PQ - 1 else P
                    for i in range(M1):
                        cols = slice(P * i, P * (i + 1))
                        last = in_parts(last_bank(i), wz_high[0:rows, q, cols], wz_low[0:rows, q, cols],
                                        z_high[0:rows, q, :], z_low[0:rows, q, :], n == 0, n == PQ)
                        if n == PQ:
                            last.then_inc(h_done, 1)

            def step(u, slot, new=True, grams=True, done=True, ahead=True):
                ending = new and plans_of(u) is END
                for i in range(PIECES):
                    if new and not ending:
                        for kind, run in plans_of(u)[slot][i]:
                            fill(u, slot, kind, run)
                    if grams:
                        gram(u if slot else u - 1, 1 - slot, i)
                    if slot == 0 and ahead and i == (PIECES - 1 if is_first(u) else 0):
                        if is_first(u):
                            pe.wait_ge(hot_idxT_ready, 2)
                        spread_indices(u + 1, 0)
                    if slot == 0 and done and i:
                        layers(u - 2, i - 1)
                    if ending:
                        for j in END_LAYERS[slot].get(i, ()):
                            layers(u - 2, j, two_banks=True)
                        for kind, run in plans_of(u)[slot][i]:
                            fill(u, slot, kind, run)

            pe.wait_ge(ident_ready, 1)
            pe.wait_ge(hot_idx_ready, 1)
            for t in range(2):
                last = pe.transpose(h_ps[0:NH, P * t:P * (t + 1)], hot_idx[:, t, :], ident[:])
            last.then_inc(hot_idx_turned, 1)
            pe.wait_ge(hot_idxT_ready, 1)
            pe.wait_ge(pick_ready, 1)
            spread_indices(0, 0)
            for t in range(2, TILES):
                c = t // 4
                last = pe.transpose(g_ps[c // 2][0:NH, c % 2, P * (t % 4):P * (t % 4 + 1)], hot_idx[:, t, :],
                                    ident[:])
            last.then_inc(hot_idx_turned, 1)

            step(0, 0, grams=False, done=False)
            pe.wait_ge(pads_zero, 1)
            step(0, 1)
            step(1, 0, done=False)
            step(1, 1)
            pe.wait_ge(weights_cut, K1 + M1)
            pe.wait_ge(small_landed, 64)
            with pe.Fori(2, UNITS - 1) as u:
                step(u, 0)
                step(u, 1)
            step(UNITS - 1, 0, done=False, ahead=False)
            step(UNITS - 1, 1)
            step(UNITS, 0, new=False, done=False, ahead=False)
            for i in range(CHUNKS + 1):
                layers(UNITS - 2, i, two_banks=True)
            last_first_layer()
            pe.wait_ge(y_copied, UNITS)
            for i in range(M1, CHUNKS + 1):
                layers(UNITS - 1, i, two_banks=True)

        def copy_pairs(engine, copy, u, parity, slot, m, members, done):
            if slot == 0 and m == 0 and not (isinstance(u, int) and u < 2):
                engine.wait_ge(z_packed, 16 * len(PACK) * (u - 1))
            engine.wait_ge(gram_done, 2 * GRAMS * u + GRAMS * slot + m + 1)
            g = g_ps[m % 2][:, :, 0:IN_BANK * WIDE].rearrange("r e (n s c) -> r e n s c", n=IN_BANK, s=GROUP)
            size = 2 * GROUP * IN_BANK
            s0 = P * slot + size * m
            zz = z[parity][:, :, s0:s0 + size].rearrange("r q (e n s) -> r s e n q", e=2, s=GROUP)
            for s in members:
                for j in range(GROUP):
                    nq = -(-(COLS - j) // GROUP)
                    last = copy(zz[ROWS * j:ROWS * j + FEATS, s, :, :, 0:nq],
                                g[ROWS * s:ROWS * s + FEATS, :, :, s, j:j + GROUP * (nq - 1) + 1:GROUP])
            last.then_inc(done, 1)

        @block.vector
        def _(dve):
            dve.memset(hot_idxT[:], 0.0).then_inc(hot_idxT_zero, 1)
            dve.memset(idx[:, TILES:, :], 0).then_inc(idx_pad_zero, 1)
            dve.wait_ge(ident_ready, 1)
            for h in range(NH):
                last = dve.tensor_copy(pick[:, h, :], ident[:, h:h + 1].to_broadcast([P, P]))
            last.then_inc(pick_ready, 1)
            dve.wait_ge(idx_landed, 16)
            for part in range(2):
                dve.tensor_copy(idx_slot[:, 0, SPAN[part]], idx[:, 0, SPAN[part]]).then_inc(idx_copied, 1)
            for h, f in enumerate(HOT):
                last = dve.tensor_copy(hot_idx[:, :, h], idx[:, 0:TILES, f])
            last.then_inc(hot_idx_ready, 1)
            for part in range(2):
                dve.tensor_copy(idx_slot[:, 1, SPAN[part]], idx[:, 1, SPAN[part]]).then_inc(idx_copied, 1)
            dve.memset(wz[:, PQ - 1, :], 0.0).then_inc(wz_zero, 1)
            dve.sem_inc(h_low_cut, 2)

            def one_hot(u, h):
                dve.wait_ge(spread, HOT_RUNS * u + h // 2 + 1)
                if not (is_first(u) and h < 2):
                    dve.wait_ge(looked_up, NH * u + max(h - 1, 0))
                here = s_ps[0:HOT_P, h % 2, :].unsqueeze(1).to_broadcast([HOT_P, HOT_ROWS, UNIT])
                rows = row_of[:].unsqueeze(2).to_broadcast([HOT_P, HOT_ROWS, UNIT])
                dve.tensor_tensor(onehot[h % 2][:], here, rows, ALU.is_equal).then_inc(onehot_ready, 1)

            def cut_table(h):
                dve.wait_ge(table_high, h + 1)
                part = hot[:, h].rearrange("p a k d -> p a (k d)")
                dve.tensor_tensor(part[:, 1, :], stage[:, h % STAGES, :], part[:, 0, :].bitcast(F32),
                                  ALU.subtract).then_inc(table_cut, 1)

            def weight_part(i):
                if i < K1 + M1:
                    high, low, whole = weight_chunk(i)
                    dve.wait_ge(weights_high, i + 1)
                    dve.tensor_tensor(low, whole, high.bitcast(F32), ALU.subtract).then_inc(weights_cut, 1)

            def cut_dense(u, parity):
                dve.wait_ge(dense_high, u + 1)
                dve.tensor_tensor(z_low[:, PQ, :], denseT[parity][:], z_high[:, PQ, :].bitcast(F32),
                                  ALU.subtract).then_inc(dense_cut, 1)

            def cut_z(u):
                dve.wait_ge(z_high_cut, u + 1)
                dve.tensor_tensor(z_low[:, 0:PQ, :], z_pack[:], z_high[:, 0:PQ, :].bitcast(F32),
                                  ALU.subtract).then_inc(z_cut, 1)

            def cut_h(u, i):
                dve.wait_ge(h_ready, CHUNKS * u + i + 1)
                dve.tensor_tensor(h1_low[:, i, :], h1[:, i % 2, :], h1_high[:, i, :].bitcast(F32),
                                  ALU.subtract).then_inc(h_low_cut, 1)

            def step(u, parity, slot, new=True, grams=True, done=True, ahead=True, cut=True, weights=False):
                at_start = is_first(u) and slot == 0
                for i in range(PIECES):
                    if new:
                        if i and not at_start:
                            for kind, run in plans_of(u)[slot][i - 1]:
                                if kind == "hot" and run + 1 < HOT_RUNS:
                                    for h in HOT_RUN[run + 1][1:]:
                                        one_hot(u + slot, h)
                        for kind, run in plans_of(u)[slot][i]:
                            if kind == "hot" and run + 1 < HOT_RUNS:
                                hs = HOT_RUN[run + 1]
                                one_hot(u + slot, hs[0])
                                if at_start:
                                    for h in hs[1:]:
                                        one_hot(u, h)
                                    for h in range(hs[-1] + 1, min(hs[-1] + 3, NH)):
                                        cut_table(h)
                    if weights:
                        weight_part(i)
                    if cut and slot and i == PIECES - 1:
                        cut_dense(u - 1, 1 - parity)
                        cut_z(u - 1)
                    if not new and i == 0:
                        cut_dense(u - 2, parity)
                        cut_z(u - 2)
                    if grams and i % 2 == 1:
                        copy_pairs(dve, dve.tensor_copy, u if slot else u - 1, parity if slot else 1 - parity, 1 - slot,
                                   i // 2, (0, 1), z_dve)
                    if slot == 0 and done and 0 < i <= M1:
                        cut_h(u - 2, i - 1)
                    if new and plans_of(u) is END:
                        for j in END_LAYERS[slot].get(i, ()):
                            if j < M1:
                                cut_h(u - 2, j)
                    if new:
                        for part, run in enumerate((FIRST - 1, NCOLD[slot] - 1)):
                            if ("cold", run) in plans_of(u)[slot][i]:
                                dve.wait_ge(turned, TURNS * u + NCOLD[0] * slot + run + 1)
                                dve.tensor_copy(idx_slot[:, slot, SPAN[part]],
                                                idx[:, bass.ds(2 * u + slot + 2, 1), SPAN[part]]
                                                .rearrange("p o f -> p (o f)")).then_inc(idx_copied, 1)
                    if slot == 0 and ahead and not at_start:
                        for h in HOT_RUN[0]:
                            if i == 2 * h + 2:
                                one_hot(u + 1, h)

            dve.wait_ge(rows_numbered, 1)
            one_hot(0, 0)
            cut_table(0)
            one_hot(0, 1)
            cut_table(1)
            cut_table(2)
            cut_table(3)
            dve.wait_ge(idx_pad_zero, 1)
            step(0, 0, 0, grams=False, done=False)
            dve.wait_ge(table_cut, NH)
            dve.memset(xT[:, :, :, FEATS:ROWS], 0.0)
            dve.memset(z_pack[:, PQ - 1, :], 0.0).then_inc(pads_zero, 1)
            dve.wait_ge(pads_zero, 1)
            one_hot(1, 0)
            one_hot(1, 1)
            step(0, 0, 1, cut=False)
            dve.wait_ge(w1_landed, 64)
            dve.tensor_tensor(wz[:, PQ, :], wz[:, PQ, :], wd2[:], ALU.add).then_inc(wd_summed, 1)
            step(1, 1, 0, done=False)
            step(1, 1, 1, weights=True)
            with dve.Fori(1, UNITS // 2 - 1) as v:
                for parity in range(2):
                    step(2 * v + parity, parity, 0)
                    step(2 * v + parity, parity, 1)
            step(UNITS - 2, 0, 0)
            step(UNITS - 2, 0, 1)
            step(UNITS - 1, 1, 0, done=False, ahead=False)
            step(UNITS - 1, 1, 1, cut=False)
            step(UNITS, 0, 0, new=False, done=False, ahead=False)
            for i in range(M1):
                cut_h(UNITS - 2, i)
            cut_dense(UNITS - 1, 1)
            for q in range(PQ):
                dve.wait_ge(z_high_cut, UNITS + q)
                dve.tensor_tensor(z_low[:, q, :], last_pack[:, q, :], z_high[:, q, :].bitcast(F32),
                                  ALU.subtract).then_inc(z_cut, 1)
            for i in range(M1):
                cut_h(UNITS - 1, i)

        @block.scalar
        def _(act):
            act.sem_inc(y_copied, 1)

            def weight_part(i):
                if i < K1 + M1:
                    high, _, whole = weight_chunk(i)
                    act.copy(high, whole).then_inc(weights_high, 1)

            def table_part(h):
                act.wait_ge(table_landed[h % STAGES], 16 * (h // STAGES + 1))
                act.copy(hot[:, h, 0].rearrange("p k d -> p (k d)"), stage[:, h % STAGES, :]).then_inc(table_high, 1)

            act.wait_ge(ident_ready, 1)
            act.copy(y_sb[:], ident[:, 0:TILES])

            act.wait_ge(hot_idxT_zero, 1)
            act.wait_ge(hot_idx_turned, 1)
            act.copy(hot_idxT[0:NH, 0:UNIT], h_ps[0:NH, 0:UNIT]).then_inc(hot_idxT_ready, 1)
            table_part(0)
            table_part(1)
            act.wait_ge(hot_idx_turned, 2)
            for c in range(TILES // 4):
                t0 = UNIT if c == 0 else 0
                last = act.copy(hot_idxT[0:NH, 4 * P * c + t0:4 * P * (c + 1)], g_ps[c // 2][0:NH, c % 2, t0:])
            last.then_inc(hot_idxT_ready, 1)
            for h in range(2, NH):
                table_part(h)
            act.dma_start(w2s[:], w2.rearrange("(m p) n -> p m n", p=P)).then_inc(small_landed, 16)
            with nc.allow_non_contiguous_dma(reason="a few hundred words, once"):
                act.dma_start(b1s[:], b1.rearrange("(m p) -> p m", p=P)).then_inc(small_landed, 16)
                act.dma_start(b2s[:], b2.rearrange("(m p) -> p m", p=P)).then_inc(small_landed, 16)
                act.dma_start(w3s[:], w3.rearrange("(m p) o -> p (m o)", p=P)).then_inc(small_landed, 16)
            act.dma_start(wd2[:], w1[D + PAIRS:2 * D + PAIRS, :]).then_inc(w1_landed, 16)
            act.dma_start(wz[:, PQ, :], w1[0:D, :]).then_inc(w1_landed, 16)
            act.dma_start(wz[:, 0:PQ - 1, :], w1[D:D + (PQ - 1) * P, :].rearrange("(q p) n -> p q n", p=P)
                          ).then_inc(w1_landed, 16)
            act.wait_ge(wz_zero, 1)
            act.dma_start(wz[0:PAIRS - (PQ - 1) * P, PQ - 1, :], w1[D + (PQ - 1) * P:D + PAIRS, :]
                          ).then_inc(w1_landed, 16)

            def cut_dense(u, parity):
                act.wait_ge(copied, number(u, 1, "cold", 0) + 1)
                act.copy(z_high[:, PQ, :], denseT[parity][:]).then_inc(dense_high, 1)

            def cut_z(u):
                act.wait_ge(z_packed, 16 * len(PACK) * (u + 1))
                act.copy(z_high[:, 0:PQ, :], z_pack[:]).then_inc(z_high_cut, 1)

            def cut_last_z(q):
                act.wait_ge(last_packed_sp[q], 16 * sum(run[0] == q for run in SP_PACK))
                act.wait_ge(last_packed_pool[q], 16 * sum(run[0] == q for run in POOL_PACK))
                act.copy(z_high[:, q, :], last_pack[:, q, :]).then_inc(z_high_cut, 1)

            def move_held(u, slot):
                act.wait_ge(copied, (last_number(0, 0, "hot") if is_first(u) else last_number(u - 1, 1, "hot")) + 1)
                h = 0
                while h < NH:
                    n = 1
                    while h + n < NH and HOT[h + n] == HOT[h] + n:
                        n += 1
                    f0 = HOT[h] + 1
                    last = act.copy(xT[:, slot, :, f0:f0 + n].rearrange("d s f -> d f s"), held[:, slot, h:h + n, :])
                    h += n
                last.then_inc(held_moved, 1)

            def layers(u, i, two_banks=False):
                out = last_bank(i) if isinstance(u, int) and u == UNITS - 1 and i < M1 else layer_bank(i, two_banks)
                if i < CHUNKS:
                    act.wait_ge(h_done, CHUNKS * u + i + 1)
                    if i < M1:
                        act.wait_ge(h_low_cut, M1 * u + i + 1)
                        act.activation(h1_high[:, i, :], out, ACT.Relu, bias=b1s[:, i:i + 1])
                        act.activation(h1[:, i % 2, :], out, ACT.Relu,
                                       bias=b1s[:, i:i + 1]).then_inc(h_ready, 1)
                    else:
                        act.activation(h2[:, i - M1, :], out, ACT.Relu,
                                       bias=b2s[:, i - M1:i - M1 + 1]).then_inc(h_ready, 1)
                else:
                    act.wait_ge(y_done, u + 1)
                    act.copy(y_sb[:, bass.ds(2 * u, 2)], h_ps[:, 0:2]).then_inc(y_copied, 1)

            def copy_bank(u, parity, slot, kind, run):
                bank = t_ps[parity_of(u, slot, kind, run)]
                if kind == "cold":
                    act.wait_ge(turned, TURNS * u + NCOLD[0] * slot + run + 1)
                    fs = COLD_RUNS[slot][run]
                    if run == 0:
                        if slot == 0 and not (isinstance(u, int) and u < 2):
                            act.wait_ge(dense_cut, u - 1)
                        act.copy(denseT[parity][:, P * slot:P * (slot + 1)], bank[:, 0, :])
                    act.copy(xT[:, slot, :, fs[0]:fs[-1] + 1].rearrange("d s f -> d f s"),
                             bank[:, 0:len(fs), :]).then_inc(copied, 1)
                else:
                    hs = HOT_RUN[run]
                    if slot:
                        act.wait_ge(held_moved, 2 * u + 2)
                    act.wait_ge(looked_up, NH * (u + slot) + hs[-1] + 1)
                    act.copy(held[:, :, hs[0]:hs[-1] + 1, :].rearrange("d a h s -> d h a s"),
                             bank[:, 0:2 * len(hs), :].rearrange("d (h a) s -> d h a s", a=2)).then_inc(copied, 1)

            def step(u, parity, slot, new=True, grams=True, done=True, cut=True, weights=False):
                at_start = is_first(u) and slot == 0
                if new and not at_start:
                    move_held(u, slot)
                ending = new and plans_of(u) is END
                for i in range(PIECES):
                    if new and not ending:
                        for kind, run in plans_of(u)[slot][i]:
                            copy_bank(u, parity, slot, kind, run)
                    if weights:
                        weight_part(i)
                    if cut and slot and i == PIECES - 1:
                        cut_dense(u - 1, 1 - parity)
                        cut_z(u - 1)
                    if not new and i == 0:
                        cut_dense(u - 2, parity)
                        cut_z(u - 2)
                    if grams and i % 2 == 1:
                        copy_pairs(act, act.copy, u if slot else u - 1, parity if slot else 1 - parity, 1 - slot,
                                   i // 2, (2, 3), z_act)
                    if slot == 0 and done and i:
                        layers(u - 2, i - 1)
                    if ending:
                        for j in END_LAYERS[slot].get(i, ()):
                            layers(u - 2, j, two_banks=True)
                        for kind, run in plans_of(u)[slot][i]:
                            copy_bank(u, parity, slot, kind, run)
                if at_start:
                    move_held(u, slot)

            step(0, 0, 0, grams=False, done=False)
            act.wait_ge(pads_zero, 1)
            step(0, 0, 1, cut=False)
            act.wait_ge(wd_summed, 1)
            act.wait_ge(small_landed, 64)
            step(1, 1, 0, done=False)
            step(1, 1, 1, weights=True)
            with act.Fori(1, UNITS // 2 - 1) as v:
                for parity in range(2):
                    step(2 * v + parity, parity, 0)
                    step(2 * v + parity, parity, 1)
            step(UNITS - 2, 0, 0)
            step(UNITS - 2, 0, 1)
            step(UNITS - 1, 1, 0, done=False)
            step(UNITS - 1, 1, 1, cut=False)
            step(UNITS, 0, 0, new=False, done=False)
            for i in range(M1):
                layers(UNITS - 2, i, two_banks=True)
            cut_dense(UNITS - 1, 1)
            cut_last_z(0)
            for i in range(M1, CHUNKS + 1):
                layers(UNITS - 2, i, two_banks=True)
            for q in range(1, PQ):
                cut_last_z(q)
            for i in range(CHUNKS + 1):
                layers(UNITS - 1, i, two_banks=True)


def kernel(**inputs):
    import numpy as _np
    import concourse.bacc as _bacc
    from concourse import mybir as _mybir
    from concourse.bass_utils import run_bass_kernel_spmd as _run

    nc = _bacc.Bacc("TRN2", target_bir_lowering=False, num_devices=1)
    arrays, aps = {}, {}
    for name, value in inputs.items():
        a = _np.ascontiguousarray(value)
        arrays[f"in_{name}"] = a
        aps[name] = nc.dram_tensor(f"in_{name}", a.shape, _mybir.dt.from_np(a.dtype), kind="ExternalInput").ap()
    n_tables = aps["ids"].shape[1]
    y = nc.dram_tensor("out_y", (aps["ids"].shape[0], 1), _mybir.dt.float32, kind="ExternalOutput").ap()
    dlrm_tower(nc, aps["r_dense_features"], aps["ids"], [aps[f"tbl_{f}"] for f in range(n_tables)],
               aps["W_top1"], aps["b_top1"], aps["W_top2"], aps["b_top2"], aps["W_top3"], y)
    r = _run(nc, [arrays], core_ids=[0])
    return r.results[0]["out_y"]
```
